# Optimizing a Trainium2 kernel written in Bass

```python
import numpy as np
import jax
import jax.numpy as jnp

def _softmax(x, axis=-1):
    return jax.nn.softmax(x, axis=axis)

def _gelu(x):
    return jax.nn.gelu(x, approximate=True)

def _silu(x):
    return jax.nn.silu(x)

def _sigmoid(x):
    return jax.nn.sigmoid(x)

def _layernorm(x, axis=-1, eps=1e-05):
    m = jnp.mean(x, axis=axis, keepdims=True)
    v = jnp.var(x, axis=axis, keepdims=True)
    return (x - m) / jnp.sqrt(v + eps)

def _scatter_add(tgt, idx, src, axis=0):
    return tgt.at[idx].add(src)

def _segment_sum(src, seg, n):
    return jax.ops.segment_sum(src, seg, n)
kernel_name = 'mk_gnn_preln_d2_gnn_r64_03459a'

def setup_inputs(seed: int=0):
    np.random.seed(seed)
    _w = jnp.asarray

    def _rec_inputs():
        import jax
        import jax.numpy as jnp
        _gk = jax.random.key(seed)
        x = -0.0005121 + 1.001 * jax.random.normal(jax.random.fold_in(_gk, 1), (50000, 64), jnp.float32)
        src = jax.random.randint(jax.random.fold_in(_gk, 2), (25000,), 0, 50000, jnp.int32)
        dst = jax.random.randint(jax.random.fold_in(_gk, 3), (25000,), 0, 50000, jnp.int32)
        _o = jnp.argsort(dst, stable=True)
        src = src[_o]
        dst = dst[_o]
        edge_attr_2 = jax.random.uniform(jax.random.fold_in(_gk, 12), (25000, 2), jnp.float32, 0.0, 1)
        edge_attr_3 = 0.00117183 + 1.0004 * jax.random.normal(jax.random.fold_in(_gk, 13), (25000, 3), jnp.float32)
        return (x, src, dst, edge_attr_2, edge_attr_3)
    x, src, dst, edge_attr_2, edge_attr_3 = _rec_inputs()

    def _L0_gnn_setup():
        import jax, jax.numpy as jnp
        import numpy as np
        K = 5

        def spline_conv(x, edge_index, pseudo, W, root, bias):
            N = x.shape[0]
            src, dst = (edge_index[0], edge_index[1])
            xk = jnp.einsum('ni,kio->nko', x, W)
            v = pseudo * (K - 1)
            bot = jnp.floor(v)
            frac = v - bot
            bot = bot.astype(jnp.int32)
            msg = jnp.zeros((src.shape[0], W.shape[2]), dtype=x.dtype)
            for s0 in (0, 1):
                for s1 in (0, 1):
                    b0 = frac[:, 0] if s0 else 1.0 - frac[:, 0]
                    b1 = frac[:, 1] if s1 else 1.0 - frac[:, 1]
                    basis = b0 * b1
                    idx = jnp.clip(bot[:, 0] + s0, 0, K - 1) + K * jnp.clip(bot[:, 1] + s1, 0, K - 1)
                    msg = msg + basis[:, None] * xk[src, idx]
            agg = jax.ops.segment_max(msg, dst, num_segments=N)
            agg = jnp.where(jnp.isfinite(agg), agg, jnp.zeros_like(agg))
            return agg + x @ root + bias
        key = jax.random.key(seed)
        ks = jax.random.split(key, 8)
        N, E, C = (50000, 25000, 64)
        Cin = C
        s = 1.0 / np.sqrt(25 * Cin)
        return {'x': jax.random.normal(ks[0], (N, C), dtype=jnp.float32), 'edge_index': jax.random.randint(ks[1], (2, E), 0, N, dtype=jnp.int32), 'edge_attr': jax.random.uniform(ks[2], (E, 2), dtype=jnp.float32), 'W1': jax.random.normal(ks[3], (25, C, C), dtype=jnp.float32) * s, 'root1': jax.random.normal(ks[4], (C, C), dtype=jnp.float32) / np.sqrt(C), 'bias1': jnp.zeros((C,), dtype=jnp.float32), 'W2': jax.random.normal(ks[5], (25, C, C), dtype=jnp.float32) * s, 'root2': jax.random.normal(ks[6], (C, C), dtype=jnp.float32) / np.sqrt(C), 'bias2': jnp.zeros((C,), dtype=jnp.float32)}
    _L0_gnn_all = _L0_gnn_setup()
    _L0_gnn_in = {k: v for k, v in _L0_gnn_all.items() if k in ('W1', 'root1', 'bias1', 'W2', 'root2', 'bias2')}
    del _L0_gnn_all

    def _L1_gnn_setup():
        import jax, jax.numpy as jnp
        import numpy as np
        M = 50000
        E = 12500
        C_IN = 64
        C_OUT = 64
        DIM = 3
        RADIUS = 1.0
        EPS = 1e-05

        def layer_norm(x, g, b):
            mu = jnp.mean(x, axis=-1, keepdims=True)
            var = jnp.mean((x - mu) ** 2, axis=-1, keepdims=True)
            return (x - mu) * jax.lax.rsqrt(var + EPS) * g + b
        key = jax.random.key(seed)
        ks = jax.random.split(key, 12)
        inv = 1.0 / np.sqrt(C_OUT)
        return {'source': jax.random.randint(ks[0], (E,), 0, M), 'target': jax.random.randint(ks[1], (E,), 0, M), 'features': jax.random.normal(ks[2], (M, C_IN), dtype=jnp.float32), 'hood_coords': jax.random.normal(ks[3], (E, DIM), dtype=jnp.float32), 'Wd1': jax.random.normal(ks[4], (DIM, C_OUT), dtype=jnp.float32) / np.sqrt(DIM), 'bd1': jnp.zeros((C_OUT,), jnp.float32), 'g1': jnp.ones((C_OUT,), jnp.float32), 'b1': jnp.zeros((C_OUT,), jnp.float32), 'Wd2': jax.random.normal(ks[5], (C_OUT, C_OUT), dtype=jnp.float32) * inv, 'bd2': jnp.zeros((C_OUT,), jnp.float32), 'g2': jnp.ones((C_OUT,), jnp.float32), 'b2': jnp.zeros((C_OUT,), jnp.float32), 'W1': jax.random.normal(ks[6], (C_IN, C_OUT), dtype=jnp.float32) / np.sqrt(C_IN), 'W2': jax.random.normal(ks[7], (C_IN, C_OUT), dtype=jnp.float32) / np.sqrt(C_IN), 'W3': jax.random.normal(ks[8], (C_IN, C_OUT), dtype=jnp.float32) / np.sqrt(C_IN)}
    _L1_gnn_all = _L1_gnn_setup()
    _L1_gnn_in = {k: v for k, v in _L1_gnn_all.items() if k in ('Wd1', 'bd1', 'g1', 'b1', 'Wd2', 'bd2', 'g2', 'b2', 'W1', 'W2', 'W3')}
    del _L1_gnn_all
    return {'x': x, 'src': src, 'dst': dst, 'edge_attr_2': edge_attr_2, 'edge_attr_3': edge_attr_3, 'L0_gnn_W1': _L0_gnn_in['W1'], 'L0_gnn_root1': _L0_gnn_in['root1'], 'L0_gnn_bias1': _L0_gnn_in['bias1'], 'L0_gnn_W2': _L0_gnn_in['W2'], 'L0_gnn_root2': _L0_gnn_in['root2'], 'L0_gnn_bias2': _L0_gnn_in['bias2'], 'L1_gnn_Wd1': _L1_gnn_in['Wd1'], 'L1_gnn_bd1': _L1_gnn_in['bd1'], 'L1_gnn_g1': _L1_gnn_in['g1'], 'L1_gnn_b1': _L1_gnn_in['b1'], 'L1_gnn_Wd2': _L1_gnn_in['Wd2'], 'L1_gnn_bd2': _L1_gnn_in['bd2'], 'L1_gnn_g2': _L1_gnn_in['g2'], 'L1_gnn_b2': _L1_gnn_in['b2'], 'L1_gnn_W1': _L1_gnn_in['W1'], 'L1_gnn_W2': _L1_gnn_in['W2'], 'L1_gnn_W3': _L1_gnn_in['W3']}

def reference(x, src, dst, edge_attr_2, edge_attr_3, L0_gnn_W1, L0_gnn_root1, L0_gnn_bias1, L0_gnn_W2, L0_gnn_root2, L0_gnn_bias2, L1_gnn_Wd1, L1_gnn_bd1, L1_gnn_g1, L1_gnn_b1, L1_gnn_Wd2, L1_gnn_bd2, L1_gnn_g2, L1_gnn_b2, L1_gnn_W1, L1_gnn_W2, L1_gnn_W3):
    import jax
    import jax.numpy as jnp

    def _L0_gnn_ref(x, edge_index, edge_attr, W1, root1, bias1, W2, root2, bias2):
        import jax, jax.numpy as jnp
        import numpy as np
        K = 5

        def spline_conv(x, edge_index, pseudo, W, root, bias):
            N = x.shape[0]
            src, dst = (edge_index[0], edge_index[1])
            xk = jnp.einsum('ni,kio->nko', x, W)
            v = pseudo * (K - 1)
            bot = jnp.floor(v)
            frac = v - bot
            bot = bot.astype(jnp.int32)
            msg = jnp.zeros((src.shape[0], W.shape[2]), dtype=x.dtype)
            for s0 in (0, 1):
                for s1 in (0, 1):
                    b0 = frac[:, 0] if s0 else 1.0 - frac[:, 0]
                    b1 = frac[:, 1] if s1 else 1.0 - frac[:, 1]
                    basis = b0 * b1
                    idx = jnp.clip(bot[:, 0] + s0, 0, K - 1) + K * jnp.clip(bot[:, 1] + s1, 0, K - 1)
                    msg = msg + basis[:, None] * xk[src, idx]
            agg = jax.ops.segment_max(msg, dst, num_segments=N)
            agg = jnp.where(jnp.isfinite(agg), agg, jnp.zeros_like(agg))
            return agg + x @ root + bias
        h = jax.nn.relu(spline_conv(x, edge_index, edge_attr, W1, root1, bias1))
        out = spline_conv(h, edge_index, edge_attr, W2, root2, bias2)
        return out

    def _L1_gnn_ref(source, target, features, hood_coords, Wd1, bd1, g1, b1, Wd2, bd2, g2, b2, W1, W2, W3):
        import jax, jax.numpy as jnp
        import numpy as np
        M = 50000
        E = 12500
        C_IN = 64
        C_OUT = 64
        DIM = 3
        RADIUS = 1.0
        EPS = 1e-05

        def layer_norm(x, g, b):
            mu = jnp.mean(x, axis=-1, keepdims=True)
            var = jnp.mean((x - mu) ** 2, axis=-1, keepdims=True)
            return (x - mu) * jax.lax.rsqrt(var + EPS) * g + b
        m = features.shape[0]
        x = hood_coords / RADIUS
        d = jax.nn.gelu(layer_norm(x @ Wd1 + bd1, g1, b1), approximate=False)
        d = jax.nn.gelu(layer_norm(d @ Wd2 + bd2, g2, b2), approximate=False)
        w1 = features @ W1
        w2 = features @ W2
        w3 = features @ W3
        logits = w1[target] - w2[source] + d
        seg_max = jax.ops.segment_max(logits, target, num_segments=m)
        seg_max = jnp.where(jnp.isfinite(seg_max), seg_max, 0.0)
        e = jnp.exp(logits - seg_max[target])
        denom = jax.ops.segment_sum(e, target, num_segments=m)
        a = e / denom[target]
        out = jax.ops.segment_sum(a * (w3[source] + d), target, num_segments=m)
        return out
    edge_index = jnp.stack([src, dst])
    h = jnp.maximum(_layernorm(x, axis=-1), 0.0)
    x = x + _L0_gnn_ref(h, edge_index, edge_attr_2, L0_gnn_W1, L0_gnn_root1, L0_gnn_bias1, L0_gnn_W2, L0_gnn_root2, L0_gnn_bias2)
    h = jnp.maximum(_layernorm(x, axis=-1), 0.0)
    x = x + _L1_gnn_ref(src, dst, h, edge_attr_3, L1_gnn_Wd1, L1_gnn_bd1, L1_gnn_g1, L1_gnn_b1, L1_gnn_Wd2, L1_gnn_bd2, L1_gnn_g2, L1_gnn_b2, L1_gnn_W1, L1_gnn_W2, L1_gnn_W3)
    return x

_drawn_inputs = setup_inputs


def setup_inputs(seed=0):
    import zlib

    import numpy as np

    out = dict(_drawn_inputs(seed))
    spreads = {'L0_gnn_bias1': (0.0, 0.1),
     'L0_gnn_bias2': (0.0, 0.1),
     'L1_gnn_bd1': (0.0, 0.1),
     'L1_gnn_g1': (1.0, 0.2),
     'L1_gnn_b1': (0.0, 0.1),
     'L1_gnn_bd2': (0.0, 0.1),
     'L1_gnn_g2': (1.0, 0.2),
     'L1_gnn_b2': (0.0, 0.1)}
    factors = {}
    for name, (base, spread) in spreads.items():
        noise = np.random.default_rng([zlib.crc32(name.encode()), seed]).standard_normal(out[name].shape)
        drawn = base * np.exp(spread * noise) if base else spread * noise
        out[name] = jnp.asarray(drawn.astype(out[name].dtype))
    for name, factor in factors.items():
        out[name] = (out[name] * factor).astype(out[name].dtype)
    return out
```

```python
from contextlib import ExitStack

import concourse.bass as bass
from concourse import mybir

F32 = mybir.dt.float32
BF16 = mybir.dt.bfloat16
I32 = mybir.dt.int32
ALU = mybir.AluOpType
ACT = mybir.ActivationFunctionType
AX = mybir.AxisListType.X

P = 128
C = 64
K = 5
TPG = 4
EG = TPG * P
NPP = 8
NG = P * NPP
KC = 3
KO = K * C
ARENA = 12800
RESTART = -(2.0 ** 127)
SKIP = 1000000.0
EPS = 1e-5


class Group:

    def __init__(self, h, off):
        self.h, self.off = h, off

    def __add__(self, d):
        return Group(self.h, self.off + d)

    def __sub__(self, d):
        return Group(self.h, self.off - d)

    @property
    def parity(self):
        return self.off % 2

    def times(self, per, plus=0):
        if self.h is None:
            return per * self.off + plus
        return self.h * (2 * per) + (per * self.off + plus)

    def uses(self, per):
        if self.h is None:
            return per * (self.off // 2 + 1)
        return self.h * per + per * (self.off // 2 + 1)

    def within(self, n):
        return self.h is not None or 0 <= self.off < n


class Steps:

    def __init__(self, sem, names):
        self.sem, self.names = sem, names.split()

    def at(self, g, name):
        return g.times(len(self.names), self.names.index(name) + 1)


def wait(eng, steps, g, name):
    value = steps.at(g, name)
    if not isinstance(value, int) or value > 0:
        eng.wait_ge(steps.sem, value)


def wait_fill(eng, sems, g, per):
    value = g.uses(per)
    if not isinstance(value, int) or value > 0:
        eng.wait_ge(sems[g.parity], value)


def build(nc, a, out):
    E = a["src"].shape[0]
    N = a["x"].shape[0]
    EGROUPS = -(-E // EG)
    NGROUPS = -(-N // NG)
    assert EGROUPS == NGROUPS and EGROUPS % 2 == 1
    G = EGROUPS
    TILES = G * TPG
    TAILP = (N - (NGROUPS - 1) * NG) // NPP
    assert TAILP * NPP == N - (NGROUPS - 1) * NG
    ROWS1 = TILES - P
    FULL1 = E // P - P
    REST = E % P

    with ExitStack() as ctx:
        def sb(name, shape, dt=F32):
            return ctx.enter_context(nc.sbuf_tensor(name, shape, dt))

        def sem(name):
            return ctx.enter_context(nc.semaphore(name))

        def pair(name):
            return [sem(name + "_even"), sem(name + "_odd")]

        def steps(name, names):
            return Steps(sem(name), names)

        T1 = nc.dram_tensor("T1", (2 * N, C), F32, kind="Internal").ap()
        T2 = nc.dram_tensor("T2", (2 * N, C), F32, kind="Internal").ap()
        restart_d = nc.dram_tensor("restart_d", (TILES * P,), BF16, kind="Internal").ap()
        T1n = T1.rearrange("(n two) c -> n (two c)", two=2)
        T2n = T2.rearrange("(n two) c -> n (two c)", two=2)

        ident = sb("ident", [P, P])
        zero = sb("zero", [P, C])
        Wk = [sb(f"Wk{i}", [P, KC, K, C]) for i in (1, 2)]
        root = [sb(f"rootpair{i}", [P, P]) for i in (1, 2)]
        bias = [sb(f"bias{i}r", [P, C]) for i in (1, 2)]
        Wd1 = sb("Wd1quad", [4 * TPG, TPG, C])
        Wd2 = sb("Wd2pair", [P, P])
        mrow = {n: sb(f"{n}r", [P, C]) for n in ("g1", "b1", "bd2", "g2", "b2")}
        Wqk = sb("Wqk", [P, 2, C])
        Wv = sb("Wv", [P, 2, C])

        srcI = sb("srcI", [P, TILES], I32)
        dstI = sb("dstI", [P, TILES], I32)
        halfI = sb("halfI", [P, TILES], I32)
        outI = sb("outI", [P, TILES], I32)
        A0 = sb("A0", [P, TILES, K])
        A1 = sb("A1", [P, TILES, K])
        E3x = sb("E3x", [P, TILES, 4])
        D = sb("D", [P, TILES, C])
        restart = sb("restart", [P, TILES * P], BF16)

        arena = sb("arena", [P, ARENA])

        class Arena:
            def __init__(self, start=0):
                self.at = start

            def take(self, shape, dt=F32):
                n = 1
                for d in shape[1:]:
                    n *= d
                words = n // 2 if dt == BF16 else n
                v = arena[0:shape[0], self.at:self.at + words]
                self.at += words
                assert self.at <= ARENA
                if dt != F32:
                    v = v.bitcast(dt)
                if len(shape) == 2:
                    return v
                if len(shape) == 3:
                    return v.rearrange("p (a b) -> p a b", a=shape[1])
                return v.rearrange("p (a b c) -> p a b c", a=shape[1], b=shape[2])

        first = Arena()
        rows_i = first.take([P, 4, 2 * P], I32)
        rows_f = first.take([P, 4, 2 * P])
        rows_r = first.take([P, 2 * P], BF16)
        ends_r = first.take([P, 2 * P])
        begins_r = first.take([P, 2 * P])
        ea2 = first.take([P, 2, P * 2])
        ea3 = first.take([P, 2, P * 3])
        vcol = first.take([P, 2, TILES])
        hat = first.take([P, TILES])
        hat2 = first.take([P, TILES])

        e3s = sb("e3s", [P, TPG, 4])
        gath = [sb(f"gath{i}", [P, TPG, 2, 2 * C]) for i in (0, 1)]
        gidx = [sb(f"gidx{i}", [P, 2 * TPG], I32) for i in (0, 1)]
        sidx = [sb(f"sidx{i}", [P, TPG], I32) for i in (0, 1)]
        srow = [sb(f"srow{i}", [P, TPG, C]) for i in (0, 1)]
        lnc = sb("lnc", [P, 2 * TPG, C])
        lnq = sb("lnq", [P, 2 * TPG, C])
        lns = sb("lns", [P, 8, 2 * TPG])
        a0r = sb("a0r", [P, TPG, K])

        msg = sb("msg", [P, TPG, C])
        nhT = sb("nhT", [P, 4 * P])
        nst = sb("nst", [P, 4, NPP])
        conv_mem = Arena()
        nx = [conv_mem.take([P, NPP, C]) for _ in (0, 1)]
        nt = [conv_mem.take([P, NPP, 2 * C]) for _ in (0, 1)]
        no = [conv_mem.take([P, NPP, C]) for _ in (0, 1)]
        nln, nq, nh = (conv_mem.take([P, NPP, C]) for _ in range(3))
        assert conv_mem.at >= first.at
        V = conv_mem.take([P, TPG, K * C])
        ZT = [conv_mem.take([P, KC, P]) for _ in (0, 1)]
        Z = [conv_mem.take([P, TPG, KC * P]) for _ in (0, 1)]
        agg = [conv_mem.take([C, EG]) for _ in (0, 1)]
        att_mem = Arena()
        x1 = [att_mem.take([P, 2 * TPG, C]) for _ in (0, 1)]
        xn = att_mem.take([P, TPG, 2 * C])
        pp, d0, lm, dm = (att_mem.take([P, EG]) for _ in range(4))
        mb = [att_mem.take([P, EG + 1]) for _ in (0, 1)]
        sums = [att_mem.take([P, EG]) for _ in (0, 1)]
        rec = att_mem.take([P, TPG, C])
        DD = [att_mem.take([P, TPG, 2 * C]) for _ in (0, 1)]
        XT = [att_mem.take([P, EG]) for _ in (0, 1)]

        turns = []
        for b, width in ((0, P), (1, ROWS1)):
            cols = slice(b * P, b * P + width)
            for q, t in ((0, srcI), (1, dstI), (2, outI), (3, halfI)):
                turns.append((rows_f[:, q, b * P:b * P + P], t[:, cols]))
            for c in (0, 1):
                turns.append((ea2[:, b, :].rearrange("t (p c) -> t c p", c=2)[:, c], vcol[:, c, cols]))
            for c in (0, 1, 2):
                turns.append((ea3[:, b, :].rearrange("t (p c) -> t c p", c=3)[:, c], E3x[:, cols, c]))
        PREP = 7
        COLS = len(turns) + 2 * K * 4
        ROW_LOADS = 16 * 19
        WEIGHTS = 16 * (2 * (K + 3) + 2 * TPG + 8 + len(mrow))

        bank = [ctx.enter_context(nc.psum_tensor(f"bank{i}", [P, 512], F32)) for i in range(8)]

        s_mem = sem("memsets")
        s_rows = sem("rows_loaded")
        s_w = sem("weights_loaded")
        s_id = sem("ident_built")
        s_prep = sem("rows_prepared")
        s_tr = sem("rows_turned")
        s_col = sem("columns_stored")
        s_neg = sem("W2_negated")
        s_rst = sem("restarts_written")
        s_rsb = sem("restarts_spread")
        s_zero = sem("halves_zeroed")
        pool_gate, pe_gate, sp_gate = sem("pool_gate"), sem("pe_gate"), sem("sp_gate")

        block = ctx.enter_context(nc.Block())

        def each(eng, step, before, after):
            first = 3
            pairs = (G - 1 - 2 - first + 1) // 2
            for g in range(-before, first):
                step(Group(None, g))
            with eng.Fori(0, pairs) as h:
                step(Group(h, first))
                step(Group(h, first + 1))
            for g in range(first + 2 * pairs, G + after):
                step(Group(None, g))

        def tiles_of(t, g):
            return t[:, bass.ds(g.times(TPG), TPG)]

        m = {
            "act": steps("mlp1_act", "copy turned root"),
            "pe": steps("mlp1_pe", "turn product"),
            "dve": steps("mlp1_dve", "sum mean cen sq var eps rstd norm scale shift"),
        }
        m2 = {
            "act": steps("mlp2_act", "copy turned root"),
            "pe": steps("mlp2_pe", "turn product"),
            "dve": steps("mlp2_dve", "bias sum mean cen sq var eps rstd norm scale shift"),
        }
        s_gelu = sem("gelu_done")

        def conv_sems(n):
            front = "sum mean cen sq var eps rstd a0r z0 z1 z2 z3" if n == 1 else "h z0 z1 z2 z3"
            node = "sum mean cen sq var eps rstd xn" if n == 1 else "xn"
            return {
                "gathered": pair(f"c{n}_gathered"), "scattered": pair(f"c{n}_scattered"),
                "gidx": steps(f"c{n}_gidx", "copy"), "sidx": steps(f"c{n}_sidx", "copy"),
                "front": steps(f"c{n}_front", front), "froot": steps(f"c{n}_froot", "root"),
                "pe": steps(f"c{n}_pe", "t0 t1 m0 t2 m1 t3 m2 m3"),
                "zt": steps(f"c{n}_zt", "zt0 zt1 zt2 zt3"),
                "comb": steps(f"c{n}_comb", "v0 v1 v2 v3 msg"),
                "mt": steps(f"c{n}_mt", "mt"), "scan": steps(f"c{n}_scan", "agg"),
                "at": steps(f"c{n}_at", "at"), "row": steps(f"c{n}_row", "row"),
                "nload": pair(f"c{n}_nload"), "nstore": pair(f"c{n}_nstore"),
                "n1": steps(f"c{n}_n1", node), "nroot": steps(f"c{n}_nroot", "root"),
                "npe": steps(f"c{n}_npe", "nt nr"), "nact": steps(f"c{n}_nact", "nts"),
                "n2": steps(f"c{n}_n2", "out" if n == 1 else "acc out"),
            }

        cs = {1: conv_sems(1), 2: conv_sems(2)}
        at = {
            "gathered": pair("a_gathered"), "scattered": pair("a_scattered"),
            "gidx": steps("a_gidx", "src dst"), "sidx": steps("a_sidx", "copy"),
            "ln": steps("a_ln", "addd adds sum mean cen sq var eps shift seed "
                        + " ".join(f"n{i}{c}" for i in range(3) for c in "abcd") + " xn"),
            "xt": steps("a_xt", "xt"), "xts": steps("a_xts", "dd xts"),
            "q": steps("a_q", "q1 q2"),
            "s1": steps("a_s1", "carry max lm step cut"), "exp": steps("a_exp", "p d0"),
            "s2": steps("a_s2", "pv scan"), "rt": steps("a_rt", "rt"),
            "fin": steps("a_fin", "rec y out"),
        }

        def scatter_done(eng, s):
            for par in (0, 1):
                eng.wait_ge(s["scattered"][par], 16 * TPG * ((G + 1 - par) // 2))

        def node_stores_done(eng, s, per):
            for par in (0, 1):
                eng.wait_ge(s["nstore"][par], per * ((G + 1 - par) // 2))

        @block.sync
        def _(sp):
            sp.wait_ge(s_mem, 7)
            for q, name in ((0, "src"), (1, "dst")):
                v = a[name]
                sp.dma_start(rows_i[:, q, 0:P], v[0:P * P].rearrange("(t p) -> t p", p=P)).then_inc(s_rows, 16)
                sp.dma_start(rows_i[0:FULL1, q, P:2 * P],
                             v[P * P:P * P + FULL1 * P].rearrange("(t p) -> t p", p=P)).then_inc(s_rows, 16)
                sp.dma_start(rows_i[FULL1:FULL1 + 1, q, P:P + REST],
                             v[E - REST:E].rearrange("(t p) -> t p", t=1)).then_inc(s_rows, 16)
            dst = a["dst"]
            sp.dma_start(rows_i[0:1, 2, 1:P], dst[0:P - 1].rearrange("(t p) -> t p", t=1)).then_inc(s_rows, 16)
            sp.dma_start(rows_i[1:P, 2, 0:P], dst[P - 1:P * P - 1].rearrange("(t p) -> t p", p=P)).then_inc(s_rows, 16)
            sp.dma_start(rows_i[0:FULL1, 2, P:2 * P],
                         dst[P * P - 1:P * P - 1 + FULL1 * P].rearrange("(t p) -> t p", p=P)).then_inc(s_rows, 16)
            sp.dma_start(rows_i[FULL1:FULL1 + 1, 2, P:P + REST],
                         dst[E - REST - 1:E - 1].rearrange("(t p) -> t p", t=1)).then_inc(s_rows, 16)
            sp.dma_start(rows_i[:, 3, 0:P], dst[1:P * P + 1].rearrange("(t p) -> t p", p=P)).then_inc(s_rows, 16)
            sp.dma_start(rows_i[0:FULL1, 3, P:2 * P],
                         dst[P * P + 1:P * P + 1 + FULL1 * P].rearrange("(t p) -> t p", p=P)).then_inc(s_rows, 16)
            sp.dma_start(rows_i[FULL1:FULL1 + 1, 3, P:P + REST - 1],
                         dst[E - REST + 1:E].rearrange("(t p) -> t p", t=1)).then_inc(s_rows, 16)
            for buf, name in ((ea2, "edge_attr_2"), (ea3, "edge_attr_3")):
                v = a[name]
                sp.dma_start(buf[:, 0], v[0:P * P, :].rearrange("(t p) c -> t (p c)", p=P)).then_inc(s_rows, 16)
                sp.dma_start(buf[0:FULL1, 1], v[P * P:P * P + FULL1 * P, :].rearrange("(t p) c -> t (p c)", p=P))\
                    .then_inc(s_rows, 16)
                sp.dma_start(buf[FULL1:FULL1 + 1, 1, 0:REST * v.shape[1]],
                             v[E - REST:E, :].rearrange("(t p) c -> t (p c)", t=1)).then_inc(s_rows, 16)
            sp.wait_ge(s_prep, PREP)
            sp.dma_start(restart_d[0:P * P].rearrange("(t p) -> t p", p=P), rows_r[:, 0:P]).then_inc(s_rst, 16)
            sp.dma_start(restart_d[P * P:TILES * P].rearrange("(t p) -> t p", p=P),
                         rows_r[0:ROWS1, P:2 * P]).then_inc(s_rst, 16)
            sp.wait_ge(s_rst, 32)
            sp.dma_start(restart[:, :], restart_d.rearrange("(a e) -> a e", a=1).broadcast_to([P, TILES * P]))\
                .then_inc(s_rsb, 16)

            ZP = 80
            for T in (T1, T2):
                sp.dma_start(T.rearrange("(p r two) c -> two p r c", p=ZP, two=2)[1],
                             zero[0:ZP, :].unsqueeze(1).broadcast_to([ZP, N // ZP, C])).then_inc(s_zero, 16)

            def node_rows(view, g):
                if g.h is None and g.off == NGROUPS - 1:
                    return view[(NGROUPS - 1) * NG:N].rearrange("(p j) c -> p j c", j=NPP), TAILP
                return view[bass.ds(g.times(NG), NG)].rearrange("(p j) c -> p j c", j=NPP), P

            sp.wait_ge(s_col, COLS)
            s = cs[1]

            def step1(g):
                if (g + 1).within(G):
                    n = g + 1
                    wait(sp, s["n1"], n - 2, "cen")
                    sp.sem_inc(sp_gate, 1)
                    rows, p = node_rows(a["x"], n)
                    sp.dma_start(nx[n.parity][0:p], rows).then_inc(s["nload"][n.parity], 16)
                if (g - 1).within(G):
                    n = g - 1
                    wait(sp, s["n2"], n, "out")
                    sp.sem_inc(sp_gate, 1)
                    rows, p = node_rows(T1n, n)
                    sp.dma_start(rows[:, :, 0:C], no[n.parity][0:p]).then_inc(s["nstore"][n.parity], 16)

            each(sp, step1, 1, 1)

            t = cs[2]
            scatter_done(sp, s)
            node_stores_done(sp, s, 16)

            def step2(g):
                if (g + 1).within(G):
                    n = g + 1
                    wait(sp, t["n1"], n - 2, "xn")
                    sp.sem_inc(sp_gate, 1)
                    wait(sp, t["n2"], n - 2, "acc")
                    sp.sem_inc(sp_gate, 1)
                    rows, p = node_rows(T1n, n)
                    sp.dma_start(nt[n.parity][0:p], rows).then_inc(t["nload"][n.parity], 16)
                    rows, p = node_rows(a["x"], n)
                    sp.dma_start(nx[n.parity][0:p], rows).then_inc(t["nload"][n.parity], 16)
                if (g - 1).within(G):
                    n = g - 1
                    wait(sp, t["n2"], n, "out")
                    sp.sem_inc(sp_gate, 1)
                    rows, p = node_rows(T2n, n)
                    sp.dma_start(rows[:, :, 0:C], no[n.parity][0:p]).then_inc(t["nstore"][n.parity], 16)
                    rows, p = node_rows(out, n)
                    sp.dma_start(rows, no[n.parity][0:p]).then_inc(t["nstore"][n.parity], 16)

            each(sp, step2, 1, 1)

        @block.gpsimd
        def _(pool):
            pool.memset(ident[:, :], 0.0).then_inc(s_id, 1)
            pool.wait_ge(s_id, 1)
            pool.affine_select(out=ident[:, :], in_=ident[:, :], compare_op=ALU.not_equal, fill=1.0, base=0,
                               pattern=[[-1, P]], channel_multiplier=1).then_inc(s_id, 1)
            half_bound = pool.to_reg(2 * N - 1)
            out_bound = pool.to_reg(N - 1)

            def gather(g, s, table, width, sets):
                for k in range(sets):
                    for j in range(TPG):
                        pool.indirect_dma_start(
                            out=gath[g.parity][:, j, k, 0:width], out_offset=None, in_=table,
                            in_offset=bass.IndirectOffsetOnAxis(gidx[g.parity][:, k * TPG + j:k * TPG + j + 1], 0),
                        ).then_inc(s["gathered"][g.parity], 16)

            def scatter(g, s, table, bound):
                for j in range(TPG):
                    pool.indirect_dma_start(
                        out=table,
                        out_offset=bass.IndirectOffsetOnAxis(sidx[g.parity][:, j:j + 1], 0),
                        in_=srow[g.parity][:, j, :], in_offset=None, bounds_check=bound, oob_is_err=False,
                    ).then_inc(s["scattered"][g.parity], 16)

            def conv(s, table, width, target, read):
                def step(g):
                    if (g + 2).within(G):
                        n = g + 2
                        wait(pool, s["gidx"], n, "copy")
                        wait(pool, s["front"], n - 2, read)
                        pool.sem_inc(pool_gate, 1)
                        gather(n, s, table, width, 1)
                    if (g - 1).within(G):
                        n = g - 1
                        if n.h is None and n.off == 0:
                            pool.wait_ge(s_zero, 32)
                        wait(pool, s["sidx"], n, "copy")
                        wait(pool, s["row"], n, "row")
                        pool.sem_inc(pool_gate, 1)
                        scatter(n, s, target, half_bound)

                each(pool, step, 2, 1)

            conv(cs[1], a["x"], C, T1, "cen")
            scatter_done(pool, cs[1])
            node_stores_done(pool, cs[1], 16)
            conv(cs[2], T1n, 2 * C, T2, "h")
            scatter_done(pool, cs[2])
            node_stores_done(pool, cs[2], 32)

            def step(g):
                if (g + 2).within(G):
                    n = g + 2
                    wait(pool, at["gidx"], n, "dst")
                    wait(pool, at["ln"], n - 2, "adds")
                    pool.sem_inc(pool_gate, 1)
                    gather(n, at, T2n, 2 * C, 2)
                if (g - 2).within(G):
                    n = g - 2
                    wait(pool, at["sidx"], n, "copy")
                    wait(pool, at["fin"], n, "out")
                    pool.sem_inc(pool_gate, 1)
                    scatter(n, at, out, out_bound)

            each(pool, step, 2, 2)
            scatter_done(pool, at)

        @block.scalar
        def _(act):
            act.wait_ge(s_mem, 7)
            for i in (0, 1):
                W = a[f"L0_gnn_W{i + 1}"]
                for k0 in range(K):
                    lo = C * (k0 % 2)
                    act.dma_start(Wk[i][lo:lo + C, k0 // 2],
                                  W.rearrange("(k1 k0) i o -> k0 i k1 o", k0=K)[k0]).then_inc(s_w, 16)
                for q in (0, 1):
                    act.dma_start(root[i][C * q:C * q + C, C * q:C * q + C], a[f"L0_gnn_root{i + 1}"])\
                        .then_inc(s_w, 16)
                act.dma_start(bias[i][:, :], a[f"L0_gnn_bias{i + 1}"].rearrange("(a c) -> a c", a=1)
                              .broadcast_to([P, C])).then_inc(s_w, 16)
            for j in range(TPG):
                act.dma_start(Wd1[4 * j:4 * j + 3, j, :], a["L1_gnn_Wd1"]).then_inc(s_w, 16)
                act.dma_start(Wd1[4 * j + 3:4 * j + 4, j, :], a["L1_gnn_bd1"].rearrange("(a c) -> a c", a=1))\
                    .then_inc(s_w, 16)
            for q in (0, 1):
                act.dma_start(Wd2[C * q:C * q + C, C * q:C * q + C], a["L1_gnn_Wd2"]).then_inc(s_w, 16)
                act.dma_start(Wqk[0:C, q, :], a["L1_gnn_W1"]).then_inc(s_w, 16)
                act.dma_start(Wqk[C:P, q, :], a["L1_gnn_W2"]).then_inc(s_w, 16)
                act.dma_start(Wv[C:P, q, :], a["L1_gnn_W3"]).then_inc(s_w, 16)
            for n, t in mrow.items():
                act.dma_start(t[:, :], a[f"L1_gnn_{n}"].rearrange("(a c) -> a c", a=1).broadcast_to([P, C]))\
                    .then_inc(s_w, 16)
            act.wait_ge(s_w, WEIGHTS)
            nc.scalar.mul(Wqk[C:P, :, :], Wqk[C:P, :, :], -1.0).then_inc(s_neg, 1)

            act.wait_ge(s_col, COLS)

            def step(g):
                if g.within(G):
                    wait(act, m["pe"], g - 1, "turn")
                    act.activation(e3s[:, :, :], tiles_of(E3x, g), ACT.Copy).then_inc(m["act"].sem, 1)
                    wait(act, m["pe"], g, "turn")
                    act.activation(nhT[0:16, 0:P], bank[0][0:16, 0:P], ACT.Copy).then_inc(m["act"].sem, 1)
                    wait(act, m["dve"], g, "eps")
                    act.activation(lns[:, 3, 0:TPG], lns[:, 2, 0:TPG], ACT.Sqrt).then_inc(m["act"].sem, 1)

            each(act, step, 0, 0)
            GP = 4
            act.wait_ge(m["dve"].sem, G * len(m["dve"].names))
            for q in range(GP):
                part = D[:, q * TILES // GP:(q + 1) * TILES // GP, :]
                act.activation(part, part, ACT.Gelu).then_inc(s_gelu, 1)
            act.wait_ge(s_gelu, GP)

            def step(g):
                if g.within(G):
                    wait(act, m2["pe"], g - 1, "turn")
                    act.activation(msg[:, :, :], tiles_of(D, g), ACT.Copy).then_inc(m2["act"].sem, 1)
                    wait(act, m2["pe"], g, "turn")
                    act.activation(nhT[:, 0:2 * P], bank[0][:, 0:2 * P], ACT.Copy).then_inc(m2["act"].sem, 1)
                    wait(act, m2["dve"], g, "eps")
                    act.activation(lns[:, 3, 0:TPG], lns[:, 2, 0:TPG], ACT.Sqrt).then_inc(m2["act"].sem, 1)

            each(act, step, 0, 0)
            act.wait_ge(m2["dve"].sem, G * len(m2["dve"].names))
            for q in range(GP):
                part = D[:, q * TILES // GP:(q + 1) * TILES // GP, :]
                act.activation(part, part, ACT.Gelu).then_inc(s_gelu, 1)

            def conv(n):
                s = cs[n]

                def step(g):
                    if (g + 2).within(G):
                        e = g + 2
                        wait_fill(act, s["gathered"], e - 2, 16 * TPG)
                        act.activation(gidx[e.parity][:, 0:TPG], tiles_of(srcI, e), ACT.Copy)\
                            .then_inc(s["gidx"].sem, 1)
                    if (g - 1).within(G):
                        e = g - 1
                        wait_fill(act, s["scattered"], e - 2, 16 * TPG)
                        act.activation(sidx[e.parity][:, :], tiles_of(halfI, e), ACT.Copy)\
                            .then_inc(s["sidx"].sem, 1)
                    if n == 1 and (g + 1).within(G):
                        wait(act, s["front"], g + 1, "eps")
                        act.activation(lns[:, 3, 0:TPG], lns[:, 2, 0:TPG], ACT.Sqrt).then_inc(s["froot"].sem, 1)
                    if n == 1 and g.within(G):
                        wait(act, s["n1"], g, "eps")
                        act.activation(nst[:, 3, :], nst[:, 2, :], ACT.Sqrt).then_inc(s["nroot"].sem, 1)
                    if g.within(G):
                        for j in range(TPG):
                            wait(act, s["pe"], g, f"t{j}")
                            act.activation(ZT[j % 2][:, :, :], bank[j % 2][:, 0:KC * P], ACT.Relu)\
                                .then_inc(s["zt"].sem, 1)
                    if (g - 1).within(G):
                        e = g - 1
                        wait(act, s["at"], e, "at")
                        act.activation(srow[e.parity][:, :, :], bank[5][:, 0:TPG * C], ACT.Copy)\
                            .then_inc(s["row"].sem, 1)
                    if g.within(G):
                        wait(act, s["npe"], g, "nt")
                        act.activation(nhT[:, :], bank[6][:, :], ACT.Relu).then_inc(s["nact"].sem, 1)

                each(act, step, 2, 1)

            conv(1)
            conv(2)

            def step(g):
                if (g + 2).within(G):
                    e = g + 2
                    wait_fill(act, at["gathered"], e - 2, 32 * TPG)
                    for k, t in ((0, srcI), (1, dstI)):
                        act.activation(gidx[e.parity][:, k * TPG:(k + 1) * TPG], tiles_of(t, e), ACT.Copy)\
                            .then_inc(at["gidx"].sem, 1)
                if (g - 1).within(G):
                    e = g - 1
                    wait_fill(act, at["scattered"], e - 2, 16 * TPG)
                    act.activation(sidx[e.parity][:, :], tiles_of(outI, e), ACT.Copy).then_inc(at["sidx"].sem, 1)
                if g.within(G):
                    wait(act, at["q"], g - 2, "q2")
                    act.activation(DD[g.parity].rearrange("p t (h c) -> p t h c", h=2),
                                   tiles_of(D, g).unsqueeze(2).broadcast_to([P, TPG, 2, C]), ACT.Copy)\
                        .then_inc(at["xts"].sem, 1)
                    wait(act, at["xt"], g, "xt")
                    act.activation(XT[g.parity][:, :], bank[g.parity][:, :], ACT.Relu).then_inc(at["xts"].sem, 1)
                    wait(act, at["s1"], g, "lm")
                    wait(act, at["s2"], g - 1, "scan")
                    act.activation(pp[:, :], lm[:, :], ACT.Exp).then_inc(at["exp"].sem, 1)
                    wait(act, at["s1"], g, "cut")
                    act.activation(d0[:, :], dm[:, :], ACT.Exp).then_inc(at["exp"].sem, 1)

            each(act, step, 2, 1)

        @block.tensor
        def _(pe):
            pe.wait_ge(s_id, 2)
            pe.wait_ge(s_prep, PREP)
            for n, (v, _) in enumerate(turns):
                if n >= 8:
                    pe.wait_ge(s_col, n - 7)
                pe.transpose(bank[n % 8][:, 0:P], v, ident[:, :]).then_inc(s_tr, 1)
            pe.wait_ge(s_w, WEIGHTS)
            pe.wait_ge(s_neg, 1)
            pe.wait_ge(s_col, COLS)

            def step(g):
                if g.within(G):
                    wait(pe, m["act"], g, "copy")
                    pe.sem_inc(pe_gate, 1)
                    pe.transpose(bank[0][0:16, 0:P], e3s[:, :, :].rearrange("p t c -> p (t c)"), ident[:, :])\
                        .then_inc(m["pe"].sem, 1)
                    wait(pe, m["act"], g, "turned")
                    wait(pe, m["dve"], g - 1, "cen")
                    pe.sem_inc(pe_gate, 1)
                    pe.matmul(bank[2][:, 0:TPG * C], nhT[0:16, 0:P], Wd1[:, :, :].rearrange("k t c -> k (t c)"),
                              start=True, stop=True).then_inc(m["pe"].sem, 1)

            each(pe, step, 0, 0)
            pe.wait_ge(s_gelu, 4)

            def step(g):
                if g.within(G):
                    wait(pe, m2["act"], g, "copy")
                    for q in (0, 1):
                        tr = pe.transpose(bank[0][:, q * P:q * P + P],
                                          msg[:, 2 * q:2 * q + 2, :].rearrange("p t c -> p (t c)"), ident[:, :])
                    tr.then_inc(m2["pe"].sem, 1)
                    wait(pe, m2["act"], g, "turned")
                    wait(pe, m2["dve"], g - 1, "bias")
                    for q in (0, 1):
                        mm = pe.matmul(bank[2][:, q * P:q * P + P], nhT[:, q * P:q * P + P], Wd2[:, :],
                                       start=True, stop=True)
                    mm.then_inc(m2["pe"].sem, 1)

            each(pe, step, 0, 0)

            def conv(n):
                s = cs[n]

                def turn_z(g, j):
                    wait(pe, s["front"], g, f"z{j}")
                    if j < 2:
                        wait(pe, s["zt"], g - 1, f"zt{j + 2}")
                    else:
                        wait(pe, s["zt"], g, f"zt{j - 2}")
                    for c in range(KC):
                        tr = pe.transpose(bank[j % 2][:, c * P:c * P + P], Z[g.parity][:, j, c * P:c * P + P],
                                          ident[:, :])
                    tr.then_inc(s["pe"].sem, 1)

                def product(g, j):
                    wait(pe, s["zt"], g, f"zt{j}")
                    if j < 2:
                        wait(pe, s["comb"], g - 1, f"v{j + 2}")
                    else:
                        wait(pe, s["comb"], g, f"v{j - 2}")
                    for c in range(KC):
                        mm = pe.matmul(bank[2 + j % 2][:, 0:KO], ZT[j % 2][:, c, :],
                                       Wk[n - 1][:, c].rearrange("p k o -> p (k o)"),
                                       start=(c == 0), stop=(c == KC - 1))
                    mm.then_inc(s["pe"].sem, 1)

                def step(g):
                    if g.within(G):
                        turn_z(g, 0)
                        turn_z(g, 1)
                        product(g, 0)
                        turn_z(g, 2)
                        product(g, 1)
                        turn_z(g, 3)
                        product(g, 2)
                        product(g, 3)
                    if (g - 1).within(G):
                        e = g - 1
                        wait(pe, s["scan"], e, "agg")
                        wait(pe, s["row"], e - 1, "row")
                        pe.sem_inc(pe_gate, 1)
                        for j in range(TPG):
                            tr = pe.transpose(bank[5][:, j * C:j * C + C], agg[e.parity][:, j * P:j * P + P],
                                              ident[0:C, 0:C])
                        tr.then_inc(s["at"].sem, 1)
                    if g.within(G):
                        wait(pe, s["n1"], g, "xn")
                        wait(pe, s["nact"], g - 1, "nts")
                        pe.sem_inc(pe_gate, 1)
                        for q in range(4):
                            tr = pe.transpose(bank[6][:, q * P:q * P + P],
                                              nh[:, 2 * q:2 * q + 2, :].rearrange("p t c -> p (t c)"), ident[:, :])
                        tr.then_inc(s["npe"].sem, 1)
                        wait(pe, s["nact"], g, "nts")
                        wait(pe, s["n2"], g - 1, "out" if n == 1 else "acc")
                        for q in range(4):
                            mm = pe.matmul(bank[7][:, q * P:q * P + P], nhT[:, q * P:q * P + P], root[n - 1][:, :],
                                           start=True, stop=True)
                        mm.then_inc(s["npe"].sem, 1)
                        wait(pe, s["comb"], g, "msg")
                        wait(pe, s["scan"], g - 1, "agg")
                        pe.sem_inc(pe_gate, 1)
                        for j in range(TPG):
                            tr = pe.transpose(bank[4][0:C, j * P:j * P + P], msg[:, j, :], ident[:, :])
                        tr.then_inc(s["mt"].sem, 1)

                each(pe, step, 0, 1)

            conv(1)
            conv(2)

            pe.wait_ge(s_gelu, 8)

            def step(g):
                if (g - 1).within(G):
                    e = g - 1
                    wait(pe, at["s2"], e, "scan")
                    wait(pe, at["fin"], e - 2, "y")
                    for j in range(TPG):
                        tr = pe.transpose(bank[6 + e.parity][:, j * P:j * P + P], sums[e.parity][:, j * P:j * P + P],
                                          ident[:, :])
                    tr.then_inc(at["rt"].sem, 1)
                if (g + 1).within(G):
                    e = g + 1
                    wait(pe, at["ln"], e, "xn")
                    wait(pe, at["xts"], e - 2, "xts")
                    pe.sem_inc(pe_gate, 1)
                    for j in range(TPG):
                        tr = pe.transpose(bank[e.parity][:, j * P:j * P + P],
                                          xn[:, j], ident[:, :])
                    tr.then_inc(at["xt"].sem, 1)
                if g.within(G):
                    wait(pe, at["xts"], g, "xts")
                    for b, W, reader, name in ((2, Wqk, "s1", "lm"), (4, Wv, "s2", "pv")):
                        wait(pe, at[reader], g - 2, name)
                        pe.matmul(bank[b + g.parity][:, :], W[:, :, :].rearrange("p t c -> p (t c)"),
                                  XT[g.parity][:, :], start=True, stop=False, skip_group_check=True)
                        for j in range(TPG):
                            mm = pe.matmul(bank[b + g.parity][:, j * P:j * P + P],
                                           DD[g.parity][:, j], ident[:, :],
                                           start=False, stop=(j == TPG - 1), skip_group_check=True)
                        mm.then_inc(at["q"].sem, 1)

            each(pe, step, 1, 1)

        @block.vector
        def _(dve):
            V_ = nc.vector
            V_.memset(rows_i[:, 0], 0).then_inc(s_mem, 1)
            V_.memset(rows_i[:, 1], int(SKIP)).then_inc(s_mem, 1)
            V_.memset(rows_i[:, 2:4], -1).then_inc(s_mem, 1)
            V_.memset(ea2[:, :, :], 0.0).then_inc(s_mem, 1)
            V_.memset(ea3[:, :, :], 0.0).then_inc(s_mem, 1)
            for t in (Wk[0][C:P, KC - 1], Wk[1][C:P, KC - 1], root[0][:, :], root[1][:, :],
                      Wd1[:, :, :], Wd2[:, :], Wv[:, :, :], agg[1]):
                V_.memset(t, 0.0)
            V_.memset(Z[0][:, :, KO:KC * P], 0.0)
            V_.memset(Z[1][:, :, KO:KC * P], 0.0)
            V_.memset(E3x[:, :, :], 1.0).then_inc(s_mem, 1)
            V_.memset(zero[:, :], 0.0).then_inc(s_mem, 1)

            n = 0

            def prep(ins):
                nonlocal n
                ins.then_inc(s_prep, 1)
                n += 1

            dve.wait_ge(s_rows, ROW_LOADS)
            dve.wait_ge(s_mem, 7)
            prep(V_.tensor_copy(rows_f[:, 0], rows_i[:, 0]))
            prep(V_.tensor_scalar(rows_f[:, 1], rows_i[:, 1], float(N - 1), None, ALU.min))
            prep(V_.tensor_tensor(begins_r, rows_i[:, 1], rows_i[:, 2], ALU.not_equal))
            dve.wait_ge(s_prep, n)
            prep(V_.tensor_scalar(rows_r[:, :], begins_r, RESTART, None, ALU.mult))
            prep(V_.tensor_tensor(ends_r, rows_i[:, 1], rows_i[:, 3], ALU.is_equal))
            dve.wait_ge(s_prep, n)
            prep(V_.scalar_tensor_tensor(out=rows_f[:, 2], in0=ends_r, scalar=SKIP, in1=rows_i[:, 1],
                                         op0=ALU.mult, op1=ALU.add))
            dve.wait_ge(s_prep, n)
            prep(V_.tensor_scalar(rows_f[:, 3], rows_f[:, 2], 2.0, 1.0, ALU.mult, ALU.add))
            assert n == PREP
            for k, (_, dest) in enumerate(turns):
                dve.wait_ge(s_tr, k + 1)
                width = dest.shape[1]
                V_.tensor_copy(dest, bank[k % 8][:, 0:width]).then_inc(s_col, 1)
            n = len(turns)

            def col(ins):
                nonlocal n
                ins.then_inc(s_col, 1)
                n += 1
                dve.wait_ge(s_col, n)

            dve.wait_ge(s_col, n)
            for d, A in ((0, A0), (1, A1)):
                for k in range(K):
                    col(V_.tensor_scalar(hat[:, :], vcol[:, d, :], float(K - 1), -float(k), ALU.mult, ALU.add))
                    col(V_.tensor_scalar(hat2[:, :], hat[:, :], -1.0, 1.0, ALU.mult, ALU.add))
                    col(V_.scalar_tensor_tensor(out=hat[:, :], in0=hat[:, :], scalar=1.0, in1=hat2[:, :],
                                                op0=ALU.add, op1=ALU.min))
                    col(V_.tensor_scalar(A[:, :, k], hat[:, :], 0.0, None, ALU.max))
            assert n == COLS
            dve.wait_ge(s_w, WEIGHTS)

            def centre(g, s, src, n, cbuf, qbuf, st):
                V_.tensor_reduce(st[:, 0, 0:n], src, AX, ALU.add).then_inc(s.sem, 1)
                wait(dve, s, g, "sum")
                V_.tensor_scalar(st[:, 1, 0:n], st[:, 0, 0:n], -1.0 / C, None, ALU.mult).then_inc(s.sem, 1)
                wait(dve, s, g, "mean")
                V_.tensor_tensor(cbuf, src, st[:, 1, 0:n].unsqueeze(2).broadcast_to([P, n, C]), ALU.add)\
                    .then_inc(s.sem, 1)
                wait(dve, s, g, "cen")
                V_.tensor_tensor(qbuf, cbuf, cbuf, ALU.mult).then_inc(s.sem, 1)
                wait(dve, s, g, "sq")
                V_.tensor_reduce(st[:, 0, 0:n], qbuf, AX, ALU.add).then_inc(s.sem, 1)
                wait(dve, s, g, "var")
                V_.tensor_scalar(st[:, 2, 0:n], st[:, 0, 0:n], 1.0 / C, EPS, ALU.mult, ALU.add).then_inc(s.sem, 1)

            def root_of(g, s, roots, name, n, st):
                wait(dve, roots, g, name)
                V_.reciprocal(st[:, 1, 0:n], st[:, 3, 0:n]).then_inc(s.sem, 1)
                wait(dve, s, g, "rstd")

            def row4(t):
                return t[:, :].unsqueeze(1).broadcast_to([P, TPG, C])

            def mlp(s, src_of, bias_row, scale_row, shift_row):
                def step(g):
                    if not g.within(G):
                        return
                    wait(dve, s["pe"], g, "product")
                    src = bank[2][:, 0:TPG * C].rearrange("p (t c) -> p t c", c=C)
                    d = s["dve"]
                    if bias_row is not None:
                        V_.tensor_tensor(lnc[:, TPG:, :], src, row4(bias_row), ALU.add).then_inc(d.sem, 1)
                        wait(dve, d, g, "bias")
                        src = lnc[:, TPG:, :]
                    c = lnc[:, 0:TPG, :]
                    centre(g, d, src, TPG, c, lnq[:, 0:TPG, :], lns)
                    root_of(g, d, s["act"], "root", TPG, lns)
                    V_.tensor_tensor(c, c, lns[:, 1, 0:TPG].unsqueeze(2).broadcast_to([P, TPG, C]), ALU.mult)\
                        .then_inc(d.sem, 1)
                    wait(dve, d, g, "norm")
                    V_.tensor_tensor(c, c, row4(scale_row), ALU.mult).then_inc(d.sem, 1)
                    wait(dve, d, g, "scale")
                    V_.tensor_tensor(tiles_of(D, g), c, row4(shift_row), ALU.add).then_inc(d.sem, 1)

                each(dve, step, 0, 0)

            mlp(m, None, None, mrow["g1"], mrow["b1"])
            dve.wait_ge(s_gelu, 4)
            mlp(m2, None, mrow["bd2"], mrow["g2"], mrow["b2"])

            dve.wait_ge(s_rsb, 16)

            def conv(n):
                s = cs[n]
                f, c_, n1, n2 = s["front"], s["comb"], s["n1"], s["n2"]

                def front(g):
                    wait_fill(dve, s["gathered"], g, 16 * TPG)
                    c = lnc[:, 0:TPG, :]
                    if n == 1:
                        centre(g, f, gath[g.parity][:, :, 0, 0:C], TPG, c, lnq[:, 0:TPG, :], lns)
                        root_of(g, f, s["froot"], "root", TPG, lns)
                        V_.tensor_tensor(a0r[:, :, :], tiles_of(A0, g),
                                         lns[:, 1, 0:TPG].unsqueeze(2).broadcast_to([P, TPG, K]), ALU.mult)\
                            .then_inc(f.sem, 1)
                        wait(dve, f, g, "a0r")
                    else:
                        wait(dve, f, g - 1, "z3")
                        V_.tensor_tensor(c, gath[g.parity][:, :, 0, 0:C], gath[g.parity][:, :, 0, C:2 * C], ALU.add)\
                            .then_inc(f.sem, 1)
                        wait(dve, f, g, "h")
                    for j in range(TPG):
                        w = a0r[:, j, :] if n == 1 else A0[:, bass.ds(g.times(TPG, j), 1), :]\
                            .rearrange("p t k -> p (t k)")
                        wait(dve, s["pe"], g - 2, f"t{j}")
                        V_.tensor_tensor(Z[g.parity][:, j, 0:KO].rearrange("p (k c) -> p k c", c=C),
                                         lnc[:, j:j + 1, :].broadcast_to([P, K, C]),
                                         w.unsqueeze(2).broadcast_to([P, K, C]), ALU.mult).then_inc(f.sem, 1)

                def scan(g):
                    wait(dve, s["mt"], g, "mt")
                    wait(dve, s["at"], g - 2, "at")
                    wait(dve, s["scan"], g - 1, "agg")
                    V_.tensor_tensor_scan(agg[g.parity][:, :], restart[0:C, bass.ds(g.times(EG), EG)],
                                          bank[4][0:C, :], agg[1 - g.parity][:, EG - 1:EG], ALU.add, ALU.max)\
                        .then_inc(s["scan"].sem, 1)

                def combine(g):
                    for j in range(TPG):
                        wait(dve, s["pe"], g, f"m{j}")
                        V_.tensor_tensor(V[:, j].rearrange("p (k o) -> p k o", o=C), bank[2 + j % 2][:, 0:KO].rearrange("p (k o) -> p k o", o=C),
                                         A1[:, bass.ds(g.times(TPG, j), 1), :].rearrange("p t k -> p (t k)")
                                         .unsqueeze(2).broadcast_to([P, K, C]), ALU.mult).then_inc(c_.sem, 1)
                    wait(dve, c_, g, "v3")
                    wait(dve, s["mt"], g - 1, "mt")
                    V_.tensor_reduce(msg[:, :, :], V.rearrange("p j (k o) -> p j o k", o=C), AX, ALU.add)\
                        .then_inc(c_.sem, 1)

                def node_in(g):
                    wait_fill(dve, s["nload"], g, 16 if n == 1 else 32)
                    wait(dve, s["npe"], g - 1, "nt")
                    if n == 1:
                        centre(g, n1, nx[g.parity][:, :, :], NPP, nln[:, :, :], nq[:, :, :], nst)
                        root_of(g, n1, s["nroot"], "root", NPP, nst)
                        V_.tensor_tensor(nh[:, :, :], nln[:, :, :],
                                         nst[:, 1, :].unsqueeze(2).broadcast_to([P, NPP, C]), ALU.mult)\
                            .then_inc(n1.sem, 1)
                    else:
                        V_.tensor_tensor(nh[:, :, :], nt[g.parity][:, :, 0:C], nt[g.parity][:, :, C:2 * C], ALU.add)\
                            .then_inc(n1.sem, 1)

                def node_out(g):
                    wait(dve, s["npe"], g, "nr")
                    wait_fill(dve, s["nstore"], g - 2, 16 if n == 1 else 32)
                    r = bank[7][:, :].rearrange("p (t c) -> p t c", c=C)
                    o = no[g.parity][:, :, :]
                    if n == 2:
                        V_.tensor_tensor(o, r, nx[g.parity][:, :, :], ALU.add).then_inc(n2.sem, 1)
                        wait(dve, n2, g, "acc")
                        r = o
                    V_.tensor_tensor(o, r, bias[n - 1][:, :].unsqueeze(1).broadcast_to([P, NPP, C]), ALU.add)\
                        .then_inc(n2.sem, 1)

                def step(g):
                    if (g + 1).within(G):
                        front(g + 1)
                    if (g - 1).within(G):
                        node_out(g - 1)
                    if g.within(G):
                        node_in(g)
                    if (g - 1).within(G):
                        scan(g - 1)
                    if g.within(G):
                        combine(g)

                each(dve, step, 1, 1)

            conv(1)
            conv(2)

            V_.memset(mb[1][:, EG:EG + 1], 0.0).then_inc(s_mem, 1)
            V_.memset(sums[1][:, EG - 1:EG], 0.0).then_inc(s_mem, 1)
            dve.wait_ge(s_mem, 9)
            ln, s1, s2, fin = at["ln"], at["s1"], at["s2"], at["fin"]

            def ends(g):
                wait_fill(dve, at["gathered"], g, 32 * TPG)
                X = x1[g.parity]
                wait(dve, fin, g - 2, "out")
                for slot, k, name in ((0, 1, "addd"), (1, 0, "adds")):
                    V_.tensor_tensor(X.rearrange("p (t e) c -> p t e c", e=2)[:, :, slot, :], gath[g.parity][:, :, k, 0:C], gath[g.parity][:, :, k, C:2 * C],
                                     ALU.add).then_inc(ln.sem, 1)
                wait(dve, ln, g, "adds")
                centre(g, ln, X, 2 * TPG, lnc[:, :, :], lnq[:, :, :],
                       lns)
                wait(dve, ln, g, "eps")
                v, y, t, u = (lns[:, k, :] for k in (2, 4, 5, 6))
                V_.tensor_scalar(t.bitcast(I32), v.bitcast(I32), 1, None, ALU.arith_shift_right).then_inc(ln.sem, 1)
                wait(dve, ln, g, "shift")
                V_.tensor_scalar(y.bitcast(I32), t.bitcast(I32), -1.0, float(0x5F3759DF), ALU.mult, ALU.add)\
                    .then_inc(ln.sem, 1)
                last = "seed"
                for i in range(3):
                    for c, args in (("a", (t, y, y, ALU.mult)), ("b", (u, t, v, ALU.mult)), ("c", None),
                                    ("d", (y, y, t, ALU.mult))):
                        wait(dve, ln, g, last)
                        if args is None:
                            V_.tensor_scalar(t, u, -0.5, 1.5, ALU.mult, ALU.add).then_inc(ln.sem, 1)
                        else:
                            V_.tensor_tensor(*args).then_inc(ln.sem, 1)
                        last = f"n{i}{c}"
                wait(dve, ln, g, last)
                wait(dve, at["xt"], g - 1, "xt")
                V_.tensor_tensor(xn.rearrange("p t (e c) -> p (t e) c", e=2), lnc[:, :, :],
                                 y.unsqueeze(2).broadcast_to([P, 2 * TPG, C]), ALU.mult).then_inc(ln.sem, 1)

            def softmax(g):
                q1, q2 = bank[2 + g.parity], bank[4 + g.parity]
                mx, before = mb[g.parity], mb[1 - g.parity]
                wait(dve, s1, g - 1, "step")
                V_.tensor_copy(mx[:, 0:1], before[:, EG:EG + 1]).then_inc(s1.sem, 1)
                wait(dve, s1, g, "carry")
                wait(dve, at["q"], g, "q1")
                cut = restart[:, bass.ds(g.times(EG), EG)]
                V_.tensor_tensor_scan(mx[:, 1:EG + 1], cut, q1[:, :], mx[:, 0:1], ALU.add, ALU.max)\
                    .then_inc(s1.sem, 1)
                wait(dve, s1, g, "max")
                wait(dve, at["exp"], g - 1, "d0")
                V_.tensor_tensor(lm[:, :], q1[:, :], mx[:, 1:EG + 1], ALU.subtract).then_inc(s1.sem, 1)
                V_.tensor_tensor(dm[:, :], mx[:, 0:EG], mx[:, 1:EG + 1], ALU.subtract).then_inc(s1.sem, 1)
                wait(dve, s1, g, "step")
                V_.tensor_tensor(dm[:, :], dm[:, :], cut, ALU.add).then_inc(s1.sem, 1)
                wait(dve, at["exp"], g, "p")
                wait(dve, at["q"], g, "q2")
                V_.tensor_tensor(pp[C:P, :], pp[C:P, :], q2[C:P, :], ALU.mult).then_inc(s2.sem, 1)
                wait(dve, s2, g, "pv")
                wait(dve, at["exp"], g, "d0")
                wait(dve, at["rt"], g - 2, "rt")
                V_.tensor_tensor_scan(sums[g.parity][:, :], d0[:, :], pp[:, :], sums[1 - g.parity][:, EG - 1:EG],
                                      ALU.mult, ALU.add).then_inc(s2.sem, 1)

            def finish(g):
                r = bank[6 + g.parity][:, :].rearrange("p (t h c) -> p t h c", h=2, c=C)
                wait(dve, at["rt"], g, "rt")
                V_.reciprocal(rec[:, :, :], r[:, :, 0, :]).then_inc(fin.sem, 1)
                wait(dve, fin, g, "rec")
                V_.tensor_tensor(rec[:, :, :], rec[:, :, :], r[:, :, 1, :], ALU.mult).then_inc(fin.sem, 1)
                wait(dve, fin, g, "y")
                wait_fill(dve, at["scattered"], g - 2, 16 * TPG)
                V_.tensor_tensor(srow[g.parity][:, :, :], rec[:, :, :], x1[g.parity].rearrange("p (t e) c -> p t e c", e=2)[:, :, 0, :], ALU.add)\
                    .then_inc(fin.sem, 1)

            def step(g):
                if (g - 1).within(G):
                    finish(g - 1)
                if (g + 1).within(G):
                    ends(g + 1)
                if g.within(G):
                    softmax(g)

            each(dve, step, 1, 1)


_INS = ["x", "src", "dst", "edge_attr_2", "edge_attr_3", "L0_gnn_W1", "L0_gnn_root1", "L0_gnn_bias1", "L0_gnn_W2",
        "L0_gnn_root2", "L0_gnn_bias2", "L1_gnn_Wd1", "L1_gnn_bd1", "L1_gnn_g1", "L1_gnn_b1", "L1_gnn_Wd2",
        "L1_gnn_bd2", "L1_gnn_g2", "L1_gnn_b2", "L1_gnn_W1", "L1_gnn_W2", "L1_gnn_W3"]


def kernel(**inputs):
    import numpy as _np
    import concourse.bacc as _bacc
    from concourse import mybir as _mybir
    from concourse.bass_utils import run_bass_kernel_spmd as _run

    nc = _bacc.Bacc("TRN2", target_bir_lowering=False, num_devices=1)
    arrays, args = {}, {}
    for name in _INS:
        v = _np.ascontiguousarray(inputs[name])
        arrays[f"in_{name}_dram"] = v
        args[name] = nc.dram_tensor(f"in_{name}_dram", v.shape, _mybir.dt.from_np(v.dtype), kind="ExternalInput").ap()
    shape = arrays["in_x_dram"].shape
    out = nc.dram_tensor("out_0_dram", shape, _mybir.dt.float32, kind="ExternalOutput").ap()
    build(nc, args, out)
    r = _run(nc, [arrays], core_ids=[0])
    return r.results[0]["out_0_dram"]
```

```python
from contextlib import ExitStack

import concourse.bass as bass
from concourse import mybir

F32 = mybir.dt.float32
BF16 = mybir.dt.bfloat16
I32 = mybir.dt.int32
ALU = mybir.AluOpType
ACT = mybir.ActivationFunctionType
AX = mybir.AxisListType.X

P = 128
C = 64
K = 5
TPG = 4
EG = TPG * P
NPP = 8
NG = P * NPP
KC = 3
KO = K * C
ARENA = 12800
RESTART = -(2.0 ** 127)
SKIP = 1000000.0
EPS = 1e-5


class Group:

    def __init__(self, h, off):
        self.h, self.off = h, off

    def __add__(self, d):
        return Group(self.h, self.off + d)

    def __sub__(self, d):
        return Group(self.h, self.off - d)

    @property
    def parity(self):
        return self.off % 2

    def times(self, per, plus=0):
        if self.h is None:
            return per * self.off + plus
        return self.h * (2 * per) + (per * self.off + plus)

    def uses(self, per):
        if self.h is None:
            return per * (self.off // 2 + 1)
        return self.h * per + per * (self.off // 2 + 1)

    def within(self, n):
        return self.h is not None or 0 <= self.off < n


class Steps:

    def __init__(self, sem, names):
        self.sem, self.names = sem, names.split()

    def at(self, g, name=None):
        if name is None:
            assert len(self.names) == 1
            name = self.names[0]
        return g.times(len(self.names), self.names.index(name) + 1)


def wait(eng, steps, g, name=None):
    value = steps.at(g, name)
    if not isinstance(value, int) or value > 0:
        eng.wait_ge(steps.sem, value)


def wait_fill(eng, sems, g, per):
    value = g.uses(per)
    if not isinstance(value, int) or value > 0:
        eng.wait_ge(sems[g.parity], value)


def build(nc, a, out):
    E = a["src"].shape[0]
    N = a["x"].shape[0]
    EGROUPS = -(-E // EG)
    NGROUPS = -(-N // NG)
    assert EGROUPS == NGROUPS and EGROUPS % 2 == 1
    G = EGROUPS
    TILES = G * TPG
    MT = 2 * TPG
    MG = -(-TILES // MT)
    TAILP = (N - (NGROUPS - 1) * NG) // NPP
    assert TAILP * NPP == N - (NGROUPS - 1) * NG
    ROWS1 = TILES - P
    FULL1 = E // P - P
    REST = E % P

    with ExitStack() as ctx:
        def sb(name, shape, dt=F32):
            return ctx.enter_context(nc.sbuf_tensor(name, shape, dt))

        def sem(name):
            return ctx.enter_context(nc.semaphore(name))

        def pair(name):
            return [sem(name + "_even"), sem(name + "_odd")]

        def steps(name, names):
            return Steps(sem(name), names)

        def signals(prefix, names):
            return {n: steps(f"{prefix}_{n}", n) for n in names.split()}

        T1 = nc.dram_tensor("T1", (2 * N, C), F32, kind="Internal").ap()
        T2 = nc.dram_tensor("T2", (2 * N, C), F32, kind="Internal").ap()
        restart_d = nc.dram_tensor("restart_d", (TILES * P,), BF16, kind="Internal").ap()
        T1n = T1.rearrange("(n two) c -> n (two c)", two=2)
        T2n = T2.rearrange("(n two) c -> n (two c)", two=2)

        ident = sb("ident", [P, P])
        zero = sb("zero", [P, C])
        Wk = [sb(f"Wk{i}", [P, KC, K, C]) for i in (1, 2)]
        root = [sb(f"rootpair{i}", [P, P]) for i in (1, 2)]
        bias = [sb(f"bias{i}r", [P, C]) for i in (1, 2)]
        Wd1 = sb("Wd1blocks", [4 * MT, MT, C])
        Wd2 = sb("Wd2blocks", [P, 2, C])
        bd2 = sb("bd2r", [P, 1, C])
        mcol = {n: sb(f"{n}c", [P, 1]) for n in ("g1", "b1", "g2", "b2")}
        wsum = sb("wsum", [P, 2, MT])
        spread = sb("spread", [P, 2, P])
        Wqk = sb("Wqk", [P, 2, C])
        Wv = sb("Wv", [P, 2, C])

        srcI = sb("srcI", [P, TILES], I32)
        dstI = sb("dstI", [P, TILES], I32)
        halfI = sb("halfI", [P, TILES], I32)
        outI = sb("outI", [P, TILES], I32)
        A0 = sb("A0", [P, TILES, K])
        A1 = sb("A1", [P, TILES, K])
        E3x = sb("E3x", [P, MG * MT, 4])
        DT = sb("DT", [P, MG * MT // 2, P])
        restart = sb("restart", [P, TILES * P], BF16)

        arena = sb("arena", [P, ARENA])

        class Arena:
            def __init__(self, start=0):
                self.at = start

            def take(self, shape, dt=F32):
                n = 1
                for d in shape[1:]:
                    n *= d
                words = n // 2 if dt == BF16 else n
                v = arena[0:shape[0], self.at:self.at + words]
                self.at += words
                assert self.at <= ARENA
                if dt != F32:
                    v = v.bitcast(dt)
                if len(shape) == 2:
                    return v
                if len(shape) == 3:
                    return v.rearrange("p (a b) -> p a b", a=shape[1])
                return v.rearrange("p (a b c) -> p a b c", a=shape[1], b=shape[2])

        first = Arena()
        rows_i = first.take([P, 4, 2 * P], I32)
        rows_f = first.take([P, 4, 2 * P])
        rows_r = first.take([P, 2 * P], BF16)
        ends_r = first.take([P, 2 * P])
        begins_r = first.take([P, 2 * P])
        ea2 = first.take([P, 2, P * 2])
        ea3 = first.take([P, 2, P * 3])
        vcol = first.take([P, 2, TILES])
        hat = first.take([P, TILES])
        hat2 = first.take([P, TILES])

        mc = Arena().take([P, MG * MT, C])
        mst = sb("mst", [P, 3, MG * MT])
        e3s = [sb(f"e3s{i}", [P, MT * 4]) for i in (0, 1)]

        gath = [sb(f"gath{i}", [P, TPG, 2, 2 * C]) for i in (0, 1)]
        gidx = [sb(f"gidx{i}", [P, 2 * TPG], I32) for i in (0, 1)]
        sidx = [sb(f"sidx{i}", [P, TPG], I32) for i in (0, 1)]
        srow = [sb(f"srow{i}", [P, TPG, C]) for i in (0, 1)]
        lnc = sb("lnc", [P, 2 * TPG, C])
        lnq = sb("lnq", [P, 2 * TPG, C])
        lns = sb("lns", [P, 8, 2 * TPG])
        a0r = sb("a0r", [P, TPG, K])
        jst = sb("jst", [P, 5, TPG + NPP])

        msg = sb("msg", [P, TPG, C])
        nhT = sb("nhT", [P, 4 * P])
        nst = sb("nst", [P, 4, NPP])
        flat = [t.rearrange("p a b c -> p (a b c)") for t in gath]
        mx = [t[:, 0:MT * C] for t in flat]
        mg = [t[:, MT * C:2 * MT * C] for t in flat]
        mq = [lnc, lnq]
        e3T = [nhT[0:4 * MT, i * P:i * P + P] for i in (0, 1)]
        conv_mem = Arena()
        nx = [conv_mem.take([P, NPP, C]) for _ in (0, 1)]
        nt = [conv_mem.take([P, NPP, 2 * C]) for _ in (0, 1)]
        no = [conv_mem.take([P, NPP, C]) for _ in (0, 1)]
        nln, nq, nh = (conv_mem.take([P, NPP, C]) for _ in range(3))
        V = conv_mem.take([P, TPG, K * C])
        ZT = [conv_mem.take([P, KC, P]) for _ in (0, 1)]
        Z = [conv_mem.take([P, TPG, KC * P]) for _ in (0, 1)]
        agg = [conv_mem.take([C, EG]) for _ in (0, 1)]
        att_mem = Arena()
        x1 = [att_mem.take([P, 2 * TPG, C]) for _ in (0, 1)]
        xn = att_mem.take([P, TPG, 2 * C])
        pp, d0, lm, dm = (att_mem.take([P, EG]) for _ in range(4))
        mb = [att_mem.take([P, EG + 1]) for _ in (0, 1)]
        sums = [att_mem.take([P, EG]) for _ in (0, 1)]
        rec = att_mem.take([P, TPG, C])
        XT = [att_mem.take([P, EG]) for _ in (0, 1)]

        turns = []
        for b, width in ((0, P), (1, ROWS1)):
            cols = slice(b * P, b * P + width)
            for q, t in ((0, srcI), (1, dstI), (2, outI), (3, halfI)):
                turns.append((rows_f[:, q, b * P:b * P + P], t[:, cols]))
            for c in (0, 1):
                turns.append((ea2[:, b, :].rearrange("t (p c) -> t c p", c=2)[:, c], vcol[:, c, cols]))
            for c in (0, 1, 2):
                turns.append((ea3[:, b, :].rearrange("t (p c) -> t c p", c=3)[:, c], E3x[:, cols, c]))
        PREP = 7
        COLS = len(turns) + 2 * K * 4
        ROW_LOADS = 16 * 19
        WEIGHTS = 16 * (2 * (K + 3) + 2 * MT + 8 + 1 + 2 * len(mcol))

        bank = [ctx.enter_context(nc.psum_tensor(f"bank{i}", [P, 512], F32)) for i in range(8)]

        s_mem = sem("memsets")
        s_rows = sem("rows_loaded")
        s_w = sem("weights_loaded")
        s_id = sem("ident_built")
        s_prep = sem("rows_prepared")
        s_tr = sem("rows_turned")
        s_col = sem("columns_stored")
        s_neg = sem("W2_negated")
        s_wc = sem("weights_centred")
        s_rst = sem("restarts_written")
        s_rsb = sem("restarts_spread")
        s_zero = sem("halves_zeroed")
        pool_gate, pe_gate, sp_gate = sem("pool_gate"), sem("pe_gate"), sem("sp_gate")

        block = ctx.enter_context(nc.Block())

        def each(eng, step, before, after, n=G, ahead=2):
            first = 3
            pairs = (n - ahead - first) // 2
            for g in range(-before, first):
                step(Group(None, g))
            with eng.Fori(0, pairs) as h:
                step(Group(h, first))
                step(Group(h, first + 1))
            for g in range(first + 2 * pairs, n + after):
                step(Group(None, g))

        def tiles_of(t, g):
            return t[:, bass.ds(g.times(TPG), TPG)]

        def half_of(g):
            return slice(g.parity * TPG, g.parity * TPG + TPG)

        m1 = signals("mlp1", "copy turn turned product square keep var")
        m2 = signals("mlp2", "norm turn gelu product keep square var")
        m3 = signals("mlp3", "norm turn gelu")
        s_mvar, s_mroot = sem("mlp_variances"), sem("mlp_roots")

        def end_of(eng, steps_, n=G):
            eng.wait_ge(steps_.sem, n * len(steps_.names))

        NEWTON = "seed " + " ".join(f"n{i}{c}" for i in range(3) for c in "abc")

        def conv_sems(n):
            s = {
                "gathered": pair(f"c{n}_gathered"), "scattered": pair(f"c{n}_scattered"),
                "nload": pair(f"c{n}_nload"), "nstore": pair(f"c{n}_nstore"),
                "z": steps(f"c{n}_z", "z0 z1 z2 z3"), "turn": steps(f"c{n}_turn", "t0 t1 t2 t3"), "prod": steps(f"c{n}_prod", "m0 m1 m2 m3"),
                "zt": steps(f"c{n}_zt", "zt0 zt1 zt2 zt3"), "comb": steps(f"c{n}_comb", "v0 v1 v2 half v3 msg"),
                "npe": steps(f"c{n}_npe", "nt nr"), "out": steps(f"c{n}_out", "out" if n == 1 else "acc out"),
                **signals(f"c{n}", "gidx sidx mt agg at row xn nts"),
            }
            if n == 1:
                s.update(signals("c1", "esum ecen esq evar nsum ncen nsq nvar root a0r"))
                s["norm"] = steps("c1_norm", "mean eps rstd")
            else:
                s.update(signals("c2", "h"))
            return s

        cs = {1: conv_sems(1), 2: conv_sems(2)}
        at = {
            "gathered": pair("a_gathered"), "scattered": pair("a_scattered"),
            "gidx": steps("a_gidx", "src dst"), "x1": steps("a_x1", "dst src"),
            "norm": steps("a_norm", "mean eps " + NEWTON), "q": steps("a_q", "q1 q2"),
            "s1": steps("a_s1", "carry max lm step cut"), "exp": steps("a_exp", "p d0"),
            "s2": steps("a_s2", "pv scan"), "fin": steps("a_fin", "rec y out"),
            **signals("a", "sidx sum cen sq var xn xt xts rt"),
        }

        def scatter_done(eng, s):
            for par in (0, 1):
                eng.wait_ge(s["scattered"][par], 16 * TPG * ((G + 1 - par) // 2))

        def node_stores_done(eng, s, per):
            for par in (0, 1):
                eng.wait_ge(s["nstore"][par], per * ((G + 1 - par) // 2))

        @block.sync
        def _(sp):
            sp.wait_ge(s_mem, 7)
            for q, name in ((0, "src"), (1, "dst")):
                v = a[name]
                sp.dma_start(rows_i[:, q, 0:P], v[0:P * P].rearrange("(t p) -> t p", p=P)).then_inc(s_rows, 16)
                sp.dma_start(rows_i[0:FULL1, q, P:2 * P],
                             v[P * P:P * P + FULL1 * P].rearrange("(t p) -> t p", p=P)).then_inc(s_rows, 16)
                sp.dma_start(rows_i[FULL1:FULL1 + 1, q, P:P + REST],
                             v[E - REST:E].rearrange("(t p) -> t p", t=1)).then_inc(s_rows, 16)
            dst = a["dst"]
            sp.dma_start(rows_i[0:1, 2, 1:P], dst[0:P - 1].rearrange("(t p) -> t p", t=1)).then_inc(s_rows, 16)
            sp.dma_start(rows_i[1:P, 2, 0:P], dst[P - 1:P * P - 1].rearrange("(t p) -> t p", p=P)).then_inc(s_rows, 16)
            sp.dma_start(rows_i[0:FULL1, 2, P:2 * P],
                         dst[P * P - 1:P * P - 1 + FULL1 * P].rearrange("(t p) -> t p", p=P)).then_inc(s_rows, 16)
            sp.dma_start(rows_i[FULL1:FULL1 + 1, 2, P:P + REST],
                         dst[E - REST - 1:E - 1].rearrange("(t p) -> t p", t=1)).then_inc(s_rows, 16)
            sp.dma_start(rows_i[:, 3, 0:P], dst[1:P * P + 1].rearrange("(t p) -> t p", p=P)).then_inc(s_rows, 16)
            sp.dma_start(rows_i[0:FULL1, 3, P:2 * P],
                         dst[P * P + 1:P * P + 1 + FULL1 * P].rearrange("(t p) -> t p", p=P)).then_inc(s_rows, 16)
            sp.dma_start(rows_i[FULL1:FULL1 + 1, 3, P:P + REST - 1],
                         dst[E - REST + 1:E].rearrange("(t p) -> t p", t=1)).then_inc(s_rows, 16)
            for buf, name in ((ea2, "edge_attr_2"), (ea3, "edge_attr_3")):
                v = a[name]
                sp.dma_start(buf[:, 0], v[0:P * P, :].rearrange("(t p) c -> t (p c)", p=P)).then_inc(s_rows, 16)
                sp.dma_start(buf[0:FULL1, 1], v[P * P:P * P + FULL1 * P, :].rearrange("(t p) c -> t (p c)", p=P))\
                    .then_inc(s_rows, 16)
                sp.dma_start(buf[FULL1:FULL1 + 1, 1, 0:REST * v.shape[1]],
                             v[E - REST:E, :].rearrange("(t p) c -> t (p c)", t=1)).then_inc(s_rows, 16)
            sp.wait_ge(s_prep, PREP)
            sp.dma_start(restart_d[0:P * P].rearrange("(t p) -> t p", p=P), rows_r[:, 0:P]).then_inc(s_rst, 16)
            sp.dma_start(restart_d[P * P:TILES * P].rearrange("(t p) -> t p", p=P),
                         rows_r[0:ROWS1, P:2 * P]).then_inc(s_rst, 16)
            sp.wait_ge(s_rst, 32)
            sp.dma_start(restart[:, :], restart_d.rearrange("(a e) -> a e", a=1).broadcast_to([P, TILES * P]))\
                .then_inc(s_rsb, 16)

            sp.wait_ge(s_w, WEIGHTS)
            ZP = 80
            for T in (T1, T2):
                sp.dma_start(T.rearrange("(p r two) c -> two p r c", p=ZP, two=2)[1],
                             zero[0:ZP, :].unsqueeze(1).broadcast_to([ZP, N // ZP, C])).then_inc(s_zero, 16)

            def node_rows(view, g):
                if g.h is None and g.off == NGROUPS - 1:
                    return view[(NGROUPS - 1) * NG:N].rearrange("(p j) c -> p j c", j=NPP), TAILP
                return view[bass.ds(g.times(NG), NG)].rearrange("(p j) c -> p j c", j=NPP), P

            end_of(sp, m3["norm"], MG)
            s = cs[1]

            def step1(g):
                if (g + 2).within(G):
                    n = g + 2
                    wait(sp, s["ncen"], n - 2)
                    sp.sem_inc(sp_gate, 1)
                    rows, p = node_rows(a["x"], n)
                    sp.dma_start(nx[n.parity][0:p], rows).then_inc(s["nload"][n.parity], 16)
                if g.within(G):
                    wait(sp, s["out"], g, "out")
                    sp.sem_inc(sp_gate, 1)
                    rows, p = node_rows(T1n, g)
                    sp.dma_start(rows[:, :, 0:C], no[g.parity][0:p]).then_inc(s["nstore"][g.parity], 16)

            each(sp, step1, 2, 0, ahead=3)

            t = cs[2]
            scatter_done(sp, s)
            node_stores_done(sp, s, 16)

            def step2(g):
                if (g + 1).within(G):
                    n = g + 1
                    wait(sp, t["xn"], n - 2)
                    sp.sem_inc(sp_gate, 1)
                    wait(sp, t["out"], n - 2, "acc")
                    sp.sem_inc(sp_gate, 1)
                    rows, p = node_rows(T1n, n)
                    sp.dma_start(nt[n.parity][0:p], rows).then_inc(t["nload"][n.parity], 16)
                    rows, p = node_rows(a["x"], n)
                    sp.dma_start(nx[n.parity][0:p], rows).then_inc(t["nload"][n.parity], 16)
                if (g - 1).within(G):
                    n = g - 1
                    wait(sp, t["out"], n, "out")
                    sp.sem_inc(sp_gate, 1)
                    rows, p = node_rows(T2n, n)
                    sp.dma_start(rows[:, :, 0:C], no[n.parity][0:p]).then_inc(t["nstore"][n.parity], 16)
                    rows, p = node_rows(out, n)
                    sp.dma_start(rows, no[n.parity][0:p]).then_inc(t["nstore"][n.parity], 16)

            each(sp, step2, 1, 1)

        @block.gpsimd
        def _(pool):
            pool.memset(ident[:, :], 0.0).then_inc(s_id, 1)
            pool.wait_ge(s_id, 1)
            pool.affine_select(out=ident[:, :], in_=ident[:, :], compare_op=ALU.not_equal, fill=1.0, base=0,
                               pattern=[[-1, P]], channel_multiplier=1).then_inc(s_id, 1)
            half_bound = pool.to_reg(2 * N - 1)
            out_bound = pool.to_reg(N - 1)

            def gather(g, s, table, width, sets):
                for k in range(sets):
                    for j in range(TPG):
                        pool.indirect_dma_start(
                            out=gath[g.parity][:, j, k, 0:width], out_offset=None, in_=table,
                            in_offset=bass.IndirectOffsetOnAxis(gidx[g.parity][:, k * TPG + j:k * TPG + j + 1], 0),
                        ).then_inc(s["gathered"][g.parity], 16)

            def scatter(g, s, table, bound):
                for j in range(TPG):
                    pool.indirect_dma_start(
                        out=table,
                        out_offset=bass.IndirectOffsetOnAxis(sidx[g.parity][:, j:j + 1], 0),
                        in_=srow[g.parity][:, j, :], in_offset=None, bounds_check=bound, oob_is_err=False,
                    ).then_inc(s["scattered"][g.parity], 16)

            def conv(s, table, width, target, read, ahead):
                def step(g):
                    if (g + ahead).within(G):
                        n = g + ahead
                        wait(pool, s["gidx"], n)
                        wait(pool, s[read], n - 2)
                        pool.sem_inc(pool_gate, 1)
                        gather(n, s, table, width, 1)
                    if (g - 1).within(G):
                        n = g - 1
                        if n.h is None and n.off == 0:
                            pool.wait_ge(s_zero, 32)
                        wait(pool, s["sidx"], n)
                        wait(pool, s["row"], n)
                        pool.sem_inc(pool_gate, 1)
                        scatter(n, s, target, half_bound)

                each(pool, step, ahead, 1, ahead=ahead)

            conv(cs[1], a["x"], C, T1, "ecen", 3)
            scatter_done(pool, cs[1])
            node_stores_done(pool, cs[1], 16)
            conv(cs[2], T1n, 2 * C, T2, "h", 2)
            scatter_done(pool, cs[2])
            node_stores_done(pool, cs[2], 32)

            def step(g):
                if (g + 3).within(G):
                    n = g + 3
                    wait(pool, at["gidx"], n, "dst")
                    wait(pool, at["x1"], n - 2, "src")
                    pool.sem_inc(pool_gate, 1)
                    gather(n, at, T2n, 2 * C, 2)
                if (g - 1).within(G):
                    n = g - 1
                    wait(pool, at["sidx"], n)
                    wait(pool, at["fin"], n, "out")
                    pool.sem_inc(pool_gate, 1)
                    scatter(n, at, out, out_bound)

            each(pool, step, 3, 1, ahead=3)
            scatter_done(pool, at)

        @block.scalar
        def _(act):
            act.wait_ge(s_mem, 7)
            for i in (0, 1):
                W = a[f"L0_gnn_W{i + 1}"]
                for k0 in range(K):
                    lo = C * (k0 % 2)
                    act.dma_start(Wk[i][lo:lo + C, k0 // 2],
                                  W.rearrange("(k1 k0) i o -> k0 i k1 o", k0=K)[k0]).then_inc(s_w, 16)
                for q in (0, 1):
                    act.dma_start(root[i][C * q:C * q + C, C * q:C * q + C], a[f"L0_gnn_root{i + 1}"])\
                        .then_inc(s_w, 16)
                act.dma_start(bias[i][:, :], a[f"L0_gnn_bias{i + 1}"].rearrange("(a c) -> a c", a=1)
                              .broadcast_to([P, C])).then_inc(s_w, 16)
            for j in range(MT):
                act.dma_start(Wd1[4 * j:4 * j + 3, j, :], a["L1_gnn_Wd1"]).then_inc(s_w, 16)
                act.dma_start(Wd1[4 * j + 3:4 * j + 4, j, :], a["L1_gnn_bd1"].rearrange("(a c) -> a c", a=1))\
                    .then_inc(s_w, 16)
            for q in (0, 1):
                act.dma_start(Wd2[C * q:C * q + C, q, :], a["L1_gnn_Wd2"]).then_inc(s_w, 16)
                act.dma_start(Wqk[0:C, q, :], a["L1_gnn_W1"]).then_inc(s_w, 16)
                act.dma_start(Wqk[C:P, q, :], a["L1_gnn_W2"]).then_inc(s_w, 16)
                act.dma_start(Wv[C:P, q, :], a["L1_gnn_W3"]).then_inc(s_w, 16)
                for n, t in mcol.items():
                    act.dma_start(t[C * q:C * q + C, :], a[f"L1_gnn_{n}"].rearrange("(c a) -> c a", a=1))\
                        .then_inc(s_w, 16)
            act.dma_start(bd2[:, 0, :], a["L1_gnn_bd2"].rearrange("(a c) -> a c", a=1).broadcast_to([P, C]))\
                .then_inc(s_w, 16)
            act.wait_ge(s_w, WEIGHTS)
            nc.scalar.mul(Wqk[C:P, :, :], Wqk[C:P, :, :], -1.0).then_inc(s_neg, 1)

            act.wait_ge(s_col, COLS)

            def step(g):
                if (g + 2).within(MG):
                    e = g + 2
                    wait(act, m1["turn"], e - 2)
                    act.activation(e3s[e.parity][:, :].rearrange("p (t c) -> p t c", c=4),
                                   E3x[:, bass.ds(e.times(MT), MT), :], ACT.Copy).then_inc(m1["copy"].sem, 1)
                if (g + 1).within(MG):
                    e = g + 1
                    wait(act, m1["turn"], e)
                    wait(act, m1["product"], e - 2)
                    act.activation(e3T[e.parity], bank[e.parity][0:4 * MT, 0:P], ACT.Copy)\
                        .then_inc(m1["turned"].sem, 1)
                if g.within(MG):
                    wait(act, m1["keep"], g)
                    wait(act, m1["var"], g - 2)
                    act.activation(mq[g.parity][:, :, :], mc[:, bass.ds(g.times(MT), MT), :], ACT.Square)\
                        .then_inc(m1["square"].sem, 1)

            each(act, step, 2, 0, MG)
            act.wait_ge(s_mvar, 1)
            act.activation(mst[:, 2, :], mst[:, 1, :], ACT.Sqrt).then_inc(s_mroot, 1)

            def step(g):
                if (g + 1).within(MG):
                    e = g + 1
                    wait(act, m2["turn"], e)
                    wait(act, m2["product"], e - 2)
                    act.activation(mg[e.parity], bank[e.parity][:, :], ACT.Gelu, scale=mcol["g1"][:, :],
                                   bias=mcol["b1"][:, :]).then_inc(m2["gelu"].sem, 1)
                if g.within(MG):
                    wait(act, m2["keep"], g)
                    wait(act, m2["var"], g - 2)
                    act.activation(mq[g.parity][:, :, :], mc[:, bass.ds(g.times(MT), MT), :], ACT.Square)\
                        .then_inc(m2["square"].sem, 1)

            each(act, step, 1, 0, MG)
            act.wait_ge(s_mvar, 2)
            act.activation(mst[:, 2, :], mst[:, 1, :], ACT.Sqrt).then_inc(s_mroot, 1)

            def step(g):
                wait(act, m3["turn"], g)
                act.activation(DT[:, bass.ds(g.times(MT // 2), MT // 2), :],
                               bank[4 + g.parity][:, :].rearrange("p (t e) -> p t e", e=P), ACT.Gelu,
                               scale=mcol["g2"][:, :], bias=mcol["b2"][:, :]).then_inc(m3["gelu"].sem, 1)

            each(act, step, 0, 0, MG)

            def conv(n):
                s = cs[n]
                ahead = 3 if n == 1 else 2

                def step(g):
                    def evacuate(g, j):
                        wait(act, s["turn"], g, f"t{j}")
                        act.activation(ZT[j % 2][:, :, :], bank[j % 2][:, 0:KC * P], ACT.Relu)\
                            .then_inc(s["zt"].sem, 1)

                    if (g + ahead).within(G):
                        e = g + ahead
                        wait_fill(act, s["gathered"], e - 2, 16 * TPG)
                        act.activation(gidx[e.parity][:, 0:TPG], tiles_of(srcI, e), ACT.Copy)\
                            .then_inc(s["gidx"].sem, 1)
                    if (g - 1).within(G):
                        e = g - 1
                        wait_fill(act, s["scattered"], e - 2, 16 * TPG)
                        act.activation(sidx[e.parity][:, :], tiles_of(halfI, e), ACT.Copy)\
                            .then_inc(s["sidx"].sem, 1)
                    if g.within(G):
                        evacuate(g, 2)
                    if n == 1 and (g + 2).within(G):
                        wait(act, s["ecen"], g + 2)
                        wait(act, s["evar"], g + 1)
                        act.activation(lnq[:, 0:TPG, :], lnc[:, half_of(g), :], ACT.Square)\
                            .then_inc(s["esq"].sem, 1)
                    if n == 1 and (g + 1).within(G):
                        wait(act, s["ncen"], g + 1)
                        wait(act, s["nvar"], g)
                        act.activation(nq[:, :, :], nln[:, :, :], ACT.Square).then_inc(s["nsq"].sem, 1)
                    if g.within(G):
                        wait(act, s["npe"], g, "nt")
                        act.activation(nhT[:, :], bank[6][:, :], ACT.Relu).then_inc(s["nts"].sem, 1)
                        evacuate(g, 3)
                    if n == 1 and ((g + 1).within(G) or (g + 2).within(G)):
                        wait(act, s["norm"], g + 2, "eps")
                        act.activation(jst[:, 4, :], jst[:, 2, :], ACT.Sqrt).then_inc(s["root"].sem, 1)
                    if (g + 1).within(G):
                        evacuate(g + 1, 0)
                        evacuate(g + 1, 1)
                    if (g - 1).within(G):
                        e = g - 1
                        wait(act, s["at"], e)
                        act.activation(srow[e.parity][:, :, :], bank[5][:, 0:TPG * C], ACT.Copy)\
                            .then_inc(s["row"].sem, 1)

                each(act, step, ahead, 1, ahead=ahead)

            conv(1)
            conv(2)

            def step(g):
                if (g - 1).within(G):
                    e = g - 1
                    wait_fill(act, at["scattered"], e - 2, 16 * TPG)
                    act.activation(sidx[e.parity][:, :], tiles_of(outI, e), ACT.Copy).then_inc(at["sidx"].sem, 1)
                if (g + 1).within(G):
                    wait(act, at["cen"], g + 1)
                    wait(act, at["var"], g)
                    act.activation(lnq[:, :, :], lnc[:, :, :], ACT.Square).then_inc(at["sq"].sem, 1)
                if (g + 3).within(G):
                    e = g + 3
                    wait_fill(act, at["gathered"], e - 2, 32 * TPG)
                    for k, t in ((0, srcI), (1, dstI)):
                        act.activation(gidx[e.parity][:, k * TPG:(k + 1) * TPG], tiles_of(t, e), ACT.Copy)\
                            .then_inc(at["gidx"].sem, 1)
                if g.within(G):
                    wait(act, at["s1"], g, "lm")
                    wait(act, at["s2"], g - 1, "scan")
                    act.activation(pp[:, :], lm[:, :], ACT.Exp).then_inc(at["exp"].sem, 1)
                    wait(act, at["s1"], g, "cut")
                    act.activation(d0[:, :], dm[:, :], ACT.Exp).then_inc(at["exp"].sem, 1)
                if (g + 1).within(G):
                    e = g + 1
                    wait(act, at["xt"], e)
                    wait(act, at["q"], e - 2, "q2")
                    act.activation(XT[e.parity][:, :], bank[e.parity][:, :], ACT.Relu).then_inc(at["xts"].sem, 1)

            each(act, step, 3, 1, ahead=3)

        @block.tensor
        def _(pe):
            pe.wait_ge(s_id, 2)
            pe.wait_ge(s_prep, PREP)
            for n, (v, _) in enumerate(turns):
                if n >= 8:
                    pe.wait_ge(s_col, n - 7)
                pe.transpose(bank[n % 8][:, 0:P], v, ident[:, :]).then_inc(s_tr, 1)
            pe.wait_ge(s_w, WEIGHTS)
            pe.wait_ge(s_neg, 1)
            pe.wait_ge(s_col, COLS)

            pe.wait_ge(s_wc, 9)

            def step(g):
                if (g + 1).within(MG):
                    e = g + 1
                    wait(pe, m1["copy"], e)
                    wait(pe, m1["turned"], e - 2)
                    pe.sem_inc(pe_gate, 1)
                    pe.transpose(bank[e.parity][0:4 * MT, 0:P], e3s[e.parity][:, :], ident[:, :])\
                        .then_inc(m1["turn"].sem, 1)
                if g.within(MG):
                    wait(pe, m1["turned"], g)
                    wait(pe, m1["keep"], g - 2)
                    pe.sem_inc(pe_gate, 1)
                    pe.matmul(bank[2 + g.parity][:, :], e3T[g.parity], Wd1[:, :, :].rearrange("k t c -> k (t c)"),
                              start=True, stop=True).then_inc(m1["product"].sem, 1)

            each(pe, step, 1, 0, MG)

            def turn_chunk(g, s, b):
                wait(pe, s["norm"], g)
                wait(pe, s["gelu"], g - 2)
                for q in range(MT // 2):
                    tr = pe.transpose(bank[b + g.parity][:, q * P:q * P + P], mx[g.parity][:, q * P:q * P + P],
                                      ident[:, :])
                tr.then_inc(s["turn"].sem, 1)

            def step(g):
                if (g + 1).within(MG):
                    turn_chunk(g + 1, m2, 0)
                if g.within(MG):
                    wait(pe, m2["gelu"], g)
                    wait(pe, m2["keep"], g - 2)
                    for q in range(MT // 2):
                        mm = pe.matmul(bank[2 + g.parity][:, q * P:q * P + P], mg[g.parity][:, q * P:q * P + P],
                                       Wd2[:, :, :].rearrange("k t c -> k (t c)"), start=True, stop=True)
                    mm.then_inc(m2["product"].sem, 1)

            each(pe, step, 1, 0, MG)
            each(pe, lambda g: turn_chunk(g, m3, 4), 0, 0, MG)

            def conv(n):
                s = cs[n]

                def turn_z(g, j):
                    wait(pe, s["z"], g, f"z{j}")
                    if j < 2:
                        wait(pe, s["zt"], g - 1, f"zt{j + 2}")
                    else:
                        wait(pe, s["zt"], g, f"zt{j - 2}")
                    for c in range(KC):
                        tr = pe.transpose(bank[j % 2][:, c * P:c * P + P], Z[g.parity][:, j, c * P:c * P + P],
                                          ident[:, :])
                    tr.then_inc(s["turn"].sem, 1)

                def product(g, j):
                    wait(pe, s["zt"], g, f"zt{j}")
                    if j < 2:
                        wait(pe, s["comb"], g - 1, f"v{j + 2}")
                    else:
                        wait(pe, s["comb"], g, f"v{j - 2}")
                    for c in range(KC):
                        mm = pe.matmul(bank[2 + j % 2][:, 0:KO], ZT[j % 2][:, c, :],
                                       Wk[n - 1][:, c].rearrange("p k o -> p (k o)"),
                                       start=(c == 0), stop=(c == KC - 1))
                    mm.then_inc(s["prod"].sem, 1)

                def step(g):
                    if g.within(G):
                        product(g, 0)
                    if (g - 1).within(G):
                        e = g - 1
                        wait(pe, s["comb"], e, "msg")
                        wait(pe, s["agg"], e - 1)
                        pe.sem_inc(pe_gate, 1)
                        for j in range(TPG):
                            tr = pe.transpose(bank[4][0:C, j * P:j * P + P], msg[:, j, :], ident[:, :])
                        tr.then_inc(s["mt"].sem, 1)
                    if g.within(G):
                        turn_z(g, 2)
                        product(g, 1)
                        wait(pe, s["xn"], g)
                        wait(pe, s["nts"], g - 1)
                        pe.sem_inc(pe_gate, 1)
                        for q in range(4):
                            tr = pe.transpose(bank[6][:, q * P:q * P + P],
                                              nh[:, 2 * q:2 * q + 2, :].rearrange("p t c -> p (t c)"), ident[:, :])
                        tr.then_inc(s["npe"].sem, 1)
                        turn_z(g, 3)
                        product(g, 2)
                    if (g + 1).within(G):
                        turn_z(g + 1, 0)
                    if g.within(G):
                        wait(pe, s["nts"], g)
                        wait(pe, s["out"], g - 1, "out" if n == 1 else "acc")
                        for q in range(4):
                            mm = pe.matmul(bank[7][:, q * P:q * P + P], nhT[:, q * P:q * P + P], root[n - 1][:, :],
                                           start=True, stop=True)
                        mm.then_inc(s["npe"].sem, 1)
                        product(g, 3)
                    if (g + 1).within(G):
                        turn_z(g + 1, 1)
                    if (g - 1).within(G):
                        e = g - 1
                        wait(pe, s["agg"], e)
                        wait(pe, s["row"], e - 1)
                        pe.sem_inc(pe_gate, 1)
                        for j in range(TPG):
                            tr = pe.transpose(bank[5][:, j * C:j * C + C], agg[e.parity][:, j * P:j * P + P],
                                              ident[0:C, 0:C])
                        tr.then_inc(s["at"].sem, 1)

                each(pe, step, 1, 1)

            conv(1)
            conv(2)

            def step(g):
                if g.within(G):
                    wait(pe, at["s2"], g, "scan")
                    wait(pe, at["fin"], g - 2, "y")
                    for j in range(TPG):
                        tr = pe.transpose(bank[6 + g.parity][:, j * P:j * P + P], sums[g.parity][:, j * P:j * P + P],
                                          ident[:, :])
                    tr.then_inc(at["rt"].sem, 1)
                if (g + 1).within(G):
                    e = g + 1
                    pairs = DT[:, bass.ds(e.times(TPG // 2), TPG // 2), :]
                    products = ((2, Wqk, "s1", "step"), (4, Wv, "s2", "pv"))
                    for b, _, reader, name in products:
                        wait(pe, at[reader], e - 2, name)
                        for j in (0, 1):
                            pe.matmul(bank[b + e.parity].rearrange("p (t h e) -> p h t e", h=2, e=P)[:, j],
                                      spread[:, j, :], pairs, start=(j == 0), stop=False, skip_group_check=True)
                    wait(pe, at["xn"], e)
                    wait(pe, at["xts"], e - 2)
                    pe.sem_inc(pe_gate, 1)
                    for j in range(TPG):
                        tr = pe.transpose(bank[e.parity][:, j * P:j * P + P], xn[:, j], ident[:, :])
                    tr.then_inc(at["xt"].sem, 1)
                    wait(pe, at["xts"], e)
                    for b, W, _, _ in products:
                        pe.matmul(bank[b + e.parity][:, :], W[:, :, :].rearrange("p t c -> p (t c)"),
                                  XT[e.parity][:, :], start=False, stop=True, skip_group_check=True)\
                            .then_inc(at["q"].sem, 1)

            each(pe, step, 1, 0)

        @block.vector
        def _(dve):
            V_ = nc.vector
            V_.memset(rows_i[:, 0], 0).then_inc(s_mem, 1)
            V_.memset(rows_i[:, 1], int(SKIP)).then_inc(s_mem, 1)
            V_.memset(rows_i[:, 2:4], -1).then_inc(s_mem, 1)
            V_.memset(ea2[:, :, :], 0.0).then_inc(s_mem, 1)
            V_.memset(ea3[:, :, :], 0.0).then_inc(s_mem, 1)
            for t in (Wk[0][C:P, KC - 1], Wk[1][C:P, KC - 1], root[0][:, :], root[1][:, :],
                      Wd1[:, :, :], Wd2[:, :, :], Wv[:, :, :], spread[:, :, :]):
                V_.memset(t, 0.0)
            V_.memset(E3x[:, :, :], 1.0).then_inc(s_mem, 1)
            V_.memset(zero[:, :], 0.0).then_inc(s_mem, 1)

            n = 0

            def prep(ins):
                nonlocal n
                ins.then_inc(s_prep, 1)
                n += 1

            dve.wait_ge(s_rows, ROW_LOADS)
            dve.wait_ge(s_mem, 7)
            prep(V_.tensor_copy(rows_f[:, 0], rows_i[:, 0]))
            prep(V_.tensor_scalar(rows_f[:, 1], rows_i[:, 1], float(N - 1), None, ALU.min))
            prep(V_.tensor_tensor(begins_r, rows_i[:, 1], rows_i[:, 2], ALU.not_equal))
            dve.wait_ge(s_prep, n)
            prep(V_.tensor_scalar(rows_r[:, :], begins_r, RESTART, None, ALU.mult))
            prep(V_.tensor_tensor(ends_r, rows_i[:, 1], rows_i[:, 3], ALU.is_equal))
            dve.wait_ge(s_prep, n)
            prep(V_.scalar_tensor_tensor(out=rows_f[:, 2], in0=ends_r, scalar=SKIP, in1=rows_i[:, 1],
                                         op0=ALU.mult, op1=ALU.add))
            dve.wait_ge(s_prep, n)
            prep(V_.tensor_scalar(rows_f[:, 3], rows_f[:, 2], 2.0, 1.0, ALU.mult, ALU.add))
            assert n == PREP
            for k, (_, dest) in enumerate(turns):
                dve.wait_ge(s_tr, k + 1)
                width = dest.shape[1]
                V_.tensor_copy(dest, bank[k % 8][:, 0:width]).then_inc(s_col, 1)
            n = len(turns)

            def col(ins):
                nonlocal n
                ins.then_inc(s_col, 1)
                n += 1
                dve.wait_ge(s_col, n)

            dve.wait_ge(s_col, n)
            for d, A in ((0, A0), (1, A1)):
                for k in range(K):
                    col(V_.tensor_scalar(hat[:, :], vcol[:, d, :], float(K - 1), -float(k), ALU.mult, ALU.add))
                    col(V_.tensor_scalar(hat2[:, :], hat[:, :], -1.0, 1.0, ALU.mult, ALU.add))
                    col(V_.scalar_tensor_tensor(out=hat[:, :], in0=hat[:, :], scalar=1.0, in1=hat2[:, :],
                                                op0=ALU.add, op1=ALU.min))
                    col(V_.tensor_scalar(A[:, :, k], hat[:, :], 0.0, None, ALU.max))
            assert n == COLS
            dve.wait_ge(s_w, WEIGHTS)

            n = 0
            for w, p, b in ((Wd1, 4 * MT, MT), (Wd2, P, 2), (bd2, P, 1)):
                total, mean = wsum[0:p, 0, 0:b], wsum[0:p, 1, 0:b]
                V_.tensor_reduce(total, w[:, :, :], AX, ALU.add).then_inc(s_wc, 1)
                dve.wait_ge(s_wc, n + 1)
                V_.tensor_scalar(mean, total, -1.0 / C, None, ALU.mult).then_inc(s_wc, 1)
                dve.wait_ge(s_wc, n + 2)
                V_.tensor_tensor(w[:, :, :], w[:, :, :], mean.unsqueeze(2).broadcast_to([p, b, C]), ALU.add)\
                    .then_inc(s_wc, 1)
                n += 3
                dve.wait_ge(s_wc, n)
            dve.wait_ge(s_id, 2)
            for q in (0, 1):
                half = slice(q * C, q * C + C)
                V_.tensor_copy(spread[half, q, :].rearrange("p (h c) -> p h c", h=2),
                               ident[half, half].unsqueeze(1).broadcast_to([C, 2, C]))

            def chunk_of(t, g):
                return t[:, bass.ds(g.times(MT), MT), :]

            def as_chunk(t):
                return t.rearrange("p (t c) -> p t c", c=C)

            def var(g, s):
                wait(dve, s["square"], g)
                V_.tensor_reduce(mst[:, 0, bass.ds(g.times(MT), MT)], mq[g.parity][:, :, :], AX, ALU.add)\
                    .then_inc(s["var"].sem, 1)

            def roots(s, n):
                end_of(dve, s["var"], MG)
                V_.tensor_scalar(mst[:, 1, :], mst[:, 0, :], 1.0 / C, EPS, ALU.mult, ALU.add).then_inc(s_mvar, 1)
                dve.wait_ge(s_mroot, n)
                V_.reciprocal(mst[:, 1, :], mst[:, 2, :]).then_inc(s_mem, 1)
                dve.wait_ge(s_mem, 7 + n)

            def norm(g, s):
                wait(dve, s["turn"], g - 2)
                V_.tensor_tensor(as_chunk(mx[g.parity]), chunk_of(mc, g),
                                 mst[:, 1, bass.ds(g.times(MT), MT)].unsqueeze(2).broadcast_to([P, MT, C]),
                                 ALU.mult).then_inc(s["norm"].sem, 1)

            def step(g):
                if g.within(MG):
                    wait(dve, m1["product"], g)
                    V_.tensor_copy(chunk_of(mc, g), as_chunk(bank[2 + g.parity][:, :]))\
                        .then_inc(m1["keep"].sem, 1)
                if (g - 1).within(MG):
                    var(g - 1, m1)

            dve.wait_ge(s_rst, 32)
            each(dve, step, 0, 1, MG)
            roots(m1, 1)

            def step(g):
                if (g + 2).within(MG):
                    norm(g + 2, m2)
                if g.within(MG):
                    wait(dve, m2["product"], g)
                    V_.tensor_tensor(chunk_of(mc, g), as_chunk(bank[2 + g.parity][:, :]),
                                     bd2[:, :, :].broadcast_to([P, MT, C]), ALU.add).then_inc(m2["keep"].sem, 1)
                if (g - 1).within(MG):
                    var(g - 1, m2)

            each(dve, step, 2, 1, MG)
            roots(m2, 2)
            each(dve, lambda g: norm(g, m3), 0, 0, MG)

            end_of(dve, m3["norm"], MG)
            V_.memset(Z[0][:, :, KO:KC * P], 0.0)
            V_.memset(Z[1][:, :, KO:KC * P], 0.0)
            V_.memset(agg[1], 0.0).then_inc(s_mem, 1)
            V_.memset(jst[:, :, :], 1.0).then_inc(s_mem, 1)
            dve.wait_ge(s_mem, 11)
            dve.wait_ge(s_rsb, 16)

            def newton(sem_, g, name, v, y, t):
                names = ["eps"] + NEWTON.split()
                wait(dve, sem_, g, names[names.index(name) - 1])
                if name == "seed":
                    ins = V_.tensor_scalar(y.bitcast(I32), v.bitcast(I32), -0.5, float(0x5F3759DF), ALU.mult, ALU.add)
                elif name[2] == "a":
                    ins = V_.tensor_tensor(t, y, y, ALU.mult)
                elif name[2] == "b":
                    ins = V_.scalar_tensor_tensor(out=t, in0=t, scalar=-0.5, in1=v, op0=ALU.mult, op1=ALU.mult)
                else:
                    ins = V_.scalar_tensor_tensor(out=y, in0=t, scalar=1.5, in1=y, op0=ALU.add, op1=ALU.mult)
                ins.then_inc(sem_.sem, 1)

            def conv(n):
                s = cs[n]
                jsum, jmean, jv, jy, jt = (jst[:, k, :] for k in range(5))

                def scaled(g):
                    wait(dve, s["norm"], g, "rstd")
                    wait(dve, s["z"], g - 1, "z3")
                    V_.tensor_tensor(a0r[:, :, :], tiles_of(A0, g),
                                     jy[:, 0:TPG].unsqueeze(2).broadcast_to([P, TPG, K]), ALU.mult)\
                        .then_inc(s["a0r"].sem, 1)

                def sum_ends(g):
                    wait_fill(dve, s["gathered"], g, 16 * TPG)
                    wait(dve, s["z"], g - 2, "z3")
                    V_.tensor_tensor(lnc[:, half_of(g), :], gath[g.parity][:, :, 0, 0:C],
                                     gath[g.parity][:, :, 0, C:2 * C], ALU.add).then_inc(s["h"].sem, 1)

                def spread_z(g, j):
                    if n == 1:
                        wait(dve, s["a0r"], g)
                        w = a0r[:, j, :]
                    else:
                        wait(dve, s["h"], g)
                        w = A0[:, bass.ds(g.times(TPG, j), 1), :].rearrange("p t k -> p (t k)")
                    wait(dve, s["turn"], g - 2, f"t{j}")
                    i = g.parity * TPG + j
                    V_.tensor_tensor(Z[g.parity][:, j, 0:KO].rearrange("p (k c) -> p k c", c=C),
                                     lnc[:, i:i + 1, :].broadcast_to([P, K, C]),
                                     w.unsqueeze(2).broadcast_to([P, K, C]), ALU.mult).then_inc(s["z"].sem, 1)

                def scan(g):
                    wait(dve, s["mt"], g)
                    wait(dve, s["at"], g - 2)
                    wait(dve, s["agg"], g - 1)
                    V_.tensor_tensor_scan(agg[g.parity][:, :], restart[0:C, bass.ds(g.times(EG), EG)],
                                          bank[4][0:C, :], agg[1 - g.parity][:, EG - 1:EG], ALU.add, ALU.max)\
                        .then_inc(s["agg"].sem, 1)

                def weigh(g, j):
                    wait(dve, s["prod"], g, f"m{j}")
                    wait(dve, s["comb"], g - 1, "msg")
                    V_.tensor_tensor(V[:, j].rearrange("p (k o) -> p k o", o=C),
                                     bank[2 + j % 2][:, 0:KO].rearrange("p (k o) -> p k o", o=C),
                                     A1[:, bass.ds(g.times(TPG, j), 1), :].rearrange("p t k -> p (t k)")
                                     .unsqueeze(2).broadcast_to([P, K, C]), ALU.mult).then_inc(s["comb"].sem, 1)

                def add_knots(g, half):
                    tiles = slice(2 * half, 2 * half + 2)
                    wait(dve, s["comb"], g, ("v1", "v3")[half])
                    wait(dve, s["mt"], g - 1)
                    V_.tensor_reduce(msg[:, tiles, :], V[:, tiles].rearrange("p j (k o) -> p j o k", o=C), AX, ALU.add)\
                        .then_inc(s["comb"].sem, 1)

                def node_in(g):
                    if n == 1:
                        wait(dve, s["norm"], g + 1, "rstd")
                        wait(dve, s["npe"], g - 1, "nt")
                        V_.tensor_tensor(nh[:, :, :], nln[:, :, :],
                                         jy[:, TPG:].unsqueeze(2).broadcast_to([P, NPP, C]), ALU.mult)\
                            .then_inc(s["xn"].sem, 1)
                    else:
                        wait_fill(dve, s["nload"], g, 32)
                        wait(dve, s["npe"], g - 1, "nt")
                        V_.tensor_tensor(nh[:, :, :], nt[g.parity][:, :, 0:C], nt[g.parity][:, :, C:2 * C], ALU.add)\
                            .then_inc(s["xn"].sem, 1)

                def node_out(g):
                    wait(dve, s["npe"], g, "nr")
                    wait_fill(dve, s["nstore"], g - 2, 16 if n == 1 else 32)
                    r = bank[7][:, :].rearrange("p (t c) -> p t c", c=C)
                    o = no[g.parity][:, :, :]
                    if n == 2:
                        V_.tensor_tensor(o, r, nx[g.parity][:, :, :], ALU.add).then_inc(s["out"].sem, 1)
                        wait(dve, s["out"], g, "acc")
                        r = o
                    V_.tensor_tensor(o, r, bias[n - 1][:, :].unsqueeze(1).broadcast_to([P, NPP, C]), ALU.add)\
                        .then_inc(s["out"].sem, 1)

                def sums(g):
                    wait(dve, s["norm"], g - 1, "eps")
                    if g.within(G):
                        wait_fill(dve, s["gathered"], g, 16 * TPG)
                        V_.tensor_reduce(jsum[:, 0:TPG], gath[g.parity][:, :, 0, 0:C], AX, ALU.add)\
                            .then_inc(s["esum"].sem, 1)
                    if (g - 1).within(G):
                        wait_fill(dve, s["nload"], g - 1, 16)
                        V_.tensor_reduce(jsum[:, TPG:], nx[1 - g.parity][:, :, :], AX, ALU.add)\
                            .then_inc(s["nsum"].sem, 1)

                def mean(g):
                    if g.within(G):
                        wait(dve, s["esum"], g)
                    if (g - 1).within(G):
                        wait(dve, s["nsum"], g - 1)
                    wait(dve, s["ecen"], g - 1)
                    wait(dve, s["ncen"], g - 2)
                    V_.tensor_scalar(jmean, jsum, -1.0 / C, None, ALU.mult).then_inc(s["norm"].sem, 1)

                def centre_rows(g):
                    wait(dve, s["norm"], g, "mean")
                    if g.within(G):
                        wait(dve, s["z"], g - 2, "z3")
                        V_.tensor_tensor(lnc[:, half_of(g), :], gath[g.parity][:, :, 0, 0:C],
                                         jmean[:, 0:TPG].unsqueeze(2).broadcast_to([P, TPG, C]), ALU.add)\
                            .then_inc(s["ecen"].sem, 1)
                    if (g - 1).within(G):
                        wait(dve, s["xn"], g - 2)
                        V_.tensor_tensor(nln[:, :, :], nx[1 - g.parity][:, :, :],
                                         jmean[:, TPG:].unsqueeze(2).broadcast_to([P, NPP, C]), ALU.add)\
                            .then_inc(s["ncen"].sem, 1)

                def variances(g):
                    if g.within(G):
                        wait(dve, s["esq"], g)
                        V_.tensor_reduce(jsum[:, 0:TPG], lnq[:, 0:TPG, :], AX, ALU.add).then_inc(s["evar"].sem, 1)
                    if (g - 1).within(G):
                        wait(dve, s["nsq"], g - 1)
                        V_.tensor_reduce(jsum[:, TPG:], nq[:, :, :], AX, ALU.add).then_inc(s["nvar"].sem, 1)

                def plus_eps(g):
                    if g.within(G):
                        wait(dve, s["evar"], g)
                    if (g - 1).within(G):
                        wait(dve, s["nvar"], g - 1)
                    V_.tensor_scalar(jv, jsum, 1.0 / C, EPS, ALU.mult, ALU.add).then_inc(s["norm"].sem, 1)

                def step(g):
                    now, ahead = g.within(G), (g + 1).within(G)
                    e = g + 2
                    stats = n == 1 and (e.within(G) or ahead)

                    def roots():
                        if stats:
                            wait(dve, s["root"], e)
                            V_.reciprocal(jy, jt).then_inc(s["norm"].sem, 1)

                    if now:
                        node_in(g)
                    if ahead:
                        if n == 1:
                            scaled(g + 1)
                        else:
                            sum_ends(g + 1)
                    if now:
                        weigh(g, 0)
                    if stats:
                        sums(e)
                    if ahead:
                        spread_z(g + 1, 0)
                    if stats:
                        mean(e)
                    if ahead:
                        spread_z(g + 1, 1)
                    if stats:
                        centre_rows(e)
                    if now:
                        weigh(g, 1)
                    if (g - 1).within(G):
                        scan(g - 1)
                    if stats:
                        variances(e)
                    if ahead:
                        spread_z(g + 1, 2)
                    if stats:
                        plus_eps(e)
                    if now:
                        weigh(g, 2)
                    if ahead:
                        spread_z(g + 1, 3)
                    if now:
                        add_knots(g, 0)
                        weigh(g, 3)
                        node_out(g)
                    roots()
                    if now:
                        add_knots(g, 1)

                each(dve, step, 2, 1)

            conv(1)
            conv(2)

            V_.memset(mb[1][:, EG:EG + 1], 0.0).then_inc(s_mem, 1)
            V_.memset(sums[1][:, EG - 1:EG], 0.0).then_inc(s_mem, 1)
            dve.wait_ge(s_mem, 13)
            s1, s2, fin, nm = at["s1"], at["s2"], at["fin"], at["norm"]
            asum, amean, av, ay, a_t = (lns[:, k, :] for k in range(5))

            def x1_ends(g):
                wait_fill(dve, at["gathered"], g, 32 * TPG)
                X = x1[g.parity].rearrange("p (t e) c -> p t e c", e=2)
                wait(dve, fin, g - 2, "out")
                for slot, k in ((0, 1), (1, 0)):
                    V_.tensor_tensor(X[:, :, slot, :], gath[g.parity][:, :, k, 0:C], gath[g.parity][:, :, k, C:2 * C],
                                     ALU.add).then_inc(at["x1"].sem, 1)

            def centre_ends(g):
                wait(dve, at["x1"], g, "src")
                wait(dve, nm, g - 1, "eps")
                V_.tensor_reduce(asum, x1[g.parity], AX, ALU.add).then_inc(at["sum"].sem, 1)
                wait(dve, at["sum"], g)
                V_.tensor_scalar(amean, asum, -1.0 / C, None, ALU.mult).then_inc(nm.sem, 1)
                wait(dve, nm, g, "mean")
                wait(dve, at["xn"], g - 1)
                V_.tensor_tensor(lnc[:, :, :], x1[g.parity], amean.unsqueeze(2).broadcast_to([P, 2 * TPG, C]),
                                 ALU.add).then_inc(at["cen"].sem, 1)

            def variance(g):
                wait(dve, at["sq"], g)
                V_.tensor_reduce(asum, lnq[:, :, :], AX, ALU.add).then_inc(at["var"].sem, 1)

            def plus_eps(g):
                wait(dve, at["var"], g)
                V_.tensor_scalar(av, asum, 1.0 / C, EPS, ALU.mult, ALU.add).then_inc(nm.sem, 1)

            def normalise(g):
                wait(dve, nm, g, "n2c")
                wait(dve, at["xt"], g - 1)
                V_.tensor_tensor(xn.rearrange("p t (e c) -> p (t e) c", e=2), lnc[:, :, :],
                                 ay.unsqueeze(2).broadcast_to([P, 2 * TPG, C]), ALU.mult).then_inc(at["xn"].sem, 1)

            def cut_of(g):
                return restart[:, bass.ds(g.times(EG), EG)]

            def running_max(g):
                mx, before = mb[g.parity], mb[1 - g.parity]
                wait(dve, s1, g - 1, "step")
                V_.tensor_copy(mx[:, 0:1], before[:, EG:EG + 1]).then_inc(s1.sem, 1)
                wait(dve, s1, g, "carry")
                wait(dve, at["q"], g, "q1")
                V_.tensor_tensor_scan(mx[:, 1:EG + 1], cut_of(g), bank[2 + g.parity][:, :], mx[:, 0:1],
                                      ALU.add, ALU.max).then_inc(s1.sem, 1)

            def below_max(g):
                wait(dve, s1, g, "max")
                wait(dve, at["exp"], g - 1, "p")
                V_.tensor_tensor(lm[:, :], bank[2 + g.parity][:, :], mb[g.parity][:, 1:EG + 1], ALU.subtract)\
                    .then_inc(s1.sem, 1)

            def fall(g):
                wait(dve, at["exp"], g - 1, "d0")
                V_.tensor_tensor(dm[:, :], mb[g.parity][:, 0:EG], mb[g.parity][:, 1:EG + 1], ALU.subtract)\
                    .then_inc(s1.sem, 1)

            def cut_fall(g):
                wait(dve, s1, g, "step")
                V_.tensor_tensor(dm[:, :], dm[:, :], cut_of(g), ALU.add).then_inc(s1.sem, 1)

            def weigh_values(g):
                wait(dve, at["exp"], g, "p")
                wait(dve, at["q"], g, "q2")
                V_.tensor_tensor(pp[C:P, :], pp[C:P, :], bank[4 + g.parity][C:P, :], ALU.mult).then_inc(s2.sem, 1)

            def running_sums(g):
                wait(dve, s2, g, "pv")
                wait(dve, at["exp"], g, "d0")
                wait(dve, at["rt"], g - 2)
                V_.tensor_tensor_scan(sums[g.parity][:, :], d0[:, :], pp[:, :], sums[1 - g.parity][:, EG - 1:EG],
                                      ALU.mult, ALU.add).then_inc(s2.sem, 1)

            def finish(g):
                r = bank[6 + g.parity][:, :].rearrange("p (t h c) -> p t h c", h=2, c=C)
                wait(dve, at["rt"], g)
                wait(dve, fin, g - 1, "out")
                V_.reciprocal(rec[:, :, :], r[:, :, 0, :]).then_inc(fin.sem, 1)
                wait(dve, fin, g, "rec")
                V_.tensor_tensor(rec[:, :, :], rec[:, :, :], r[:, :, 1, :], ALU.mult).then_inc(fin.sem, 1)
                wait(dve, fin, g, "y")
                wait_fill(dve, at["scattered"], g - 2, 16 * TPG)
                V_.tensor_tensor(srow[g.parity][:, :, :], rec[:, :, :],
                                 x1[g.parity].rearrange("p (t e) c -> p t e c", e=2)[:, :, 0, :], ALU.add)\
                    .then_inc(fin.sem, 1)

            def step(g):
                now, ahead = g.within(G), (g + 1).within(G)
                e = g + 1

                def refine(*names):
                    if ahead:
                        for k in names:
                            newton(nm, e, k, av, ay, a_t)

                if (g - 1).within(G):
                    finish(g - 1)
                if ahead:
                    x1_ends(e)
                    centre_ends(e)
                if now:
                    running_max(g)
                    below_max(g)
                if ahead:
                    variance(e)
                if now:
                    fall(g)
                if ahead:
                    plus_eps(e)
                if now:
                    cut_fall(g)
                refine("seed", "n0a")
                if now:
                    weigh_values(g)
                refine("n0b", "n0c", "n1a")
                if now:
                    running_sums(g)
                refine("n1b", "n1c", "n2a", "n2b", "n2c")
                if ahead:
                    normalise(e)

            each(dve, step, 1, 1)


_INS = ["x", "src", "dst", "edge_attr_2", "edge_attr_3", "L0_gnn_W1", "L0_gnn_root1", "L0_gnn_bias1", "L0_gnn_W2",
        "L0_gnn_root2", "L0_gnn_bias2", "L1_gnn_Wd1", "L1_gnn_bd1", "L1_gnn_g1", "L1_gnn_b1", "L1_gnn_Wd2",
        "L1_gnn_bd2", "L1_gnn_g2", "L1_gnn_b2", "L1_gnn_W1", "L1_gnn_W2", "L1_gnn_W3"]


def kernel(**inputs):
    import numpy as _np
    import concourse.bacc as _bacc
    from concourse import mybir as _mybir
    from concourse.bass_utils import run_bass_kernel_spmd as _run

    nc = _bacc.Bacc("TRN2", target_bir_lowering=False, num_devices=1)
    arrays, args = {}, {}
    for name in _INS:
        v = _np.ascontiguousarray(inputs[name])
        arrays[f"in_{name}_dram"] = v
        args[name] = nc.dram_tensor(f"in_{name}_dram", v.shape, _mybir.dt.from_np(v.dtype), kind="ExternalInput").ap()
    shape = arrays["in_x_dram"].shape
    out = nc.dram_tensor("out_0_dram", shape, _mybir.dt.float32, kind="ExternalOutput").ap()
    build(nc, args, out)
    r = _run(nc, [arrays], core_ids=[0])
    return r.results[0]["out_0_dram"]
```

```python
from contextlib import ExitStack

import concourse.bass as bass
from concourse import mybir

F32 = mybir.dt.float32
BF16 = mybir.dt.bfloat16
I32 = mybir.dt.int32
ALU = mybir.AluOpType
ACT = mybir.ActivationFunctionType
AX = mybir.AxisListType.X

P = 128
C = 64
K = 5
TPG = 4
EG = TPG * P
NPP = 8
NG = P * NPP
KC = 3
KO = K * C
ARENA = 12800
RESTART = -(2.0 ** 127)
SKIP = 1000000.0
EPS = 1e-5
UNROLL = 4


class Group:

    def __init__(self, h, off):
        self.h, self.off = h, off

    def __add__(self, d):
        return Group(self.h, self.off + d)

    def __sub__(self, d):
        return Group(self.h, self.off - d)

    @property
    def parity(self):
        return self.off % 2

    def times(self, per, plus=0):
        if self.h is None:
            return per * self.off + plus
        return self.h * (UNROLL * per) + (per * self.off + plus)

    def uses(self, per):
        fillings = per * (self.off // 2 + 1)
        return fillings if self.h is None else self.h * (UNROLL // 2 * per) + fillings

    def within(self, n, first=0):
        return self.h is not None or first <= self.off < n


class Steps:

    def __init__(self, sem, names):
        self.sem, self.names = sem, names.split()

    def at(self, g, name=None):
        if name is None:
            assert len(self.names) == 1
            name = self.names[0]
        return g.times(len(self.names), self.names.index(name) + 1)


def wait(eng, steps, g, name=None):
    value = steps.at(g, name)
    if not isinstance(value, int) or value > 0:
        eng.wait_ge(steps.sem, value)


def wait_fill(eng, sems, g, per):
    value = g.uses(per)
    if not isinstance(value, int) or value > 0:
        eng.wait_ge(sems[g.parity], value)


def build(nc, a, out):
    E = a["src"].shape[0]
    N = a["x"].shape[0]
    EGROUPS = -(-E // EG)
    NGROUPS = -(-N // NG)
    assert EGROUPS == NGROUPS and EGROUPS % 2 == 1
    G = EGROUPS
    TILES = G * TPG
    MT = 2 * TPG
    MG = -(-TILES // MT)
    LAYER2 = ((0, MG - 6), (MG - 6, MG))
    TAILP = (N - (NGROUPS - 1) * NG) // NPP
    assert TAILP * NPP == N - (NGROUPS - 1) * NG
    ROWS1 = TILES - P
    FULL1 = E // P - P
    REST = E % P

    with ExitStack() as ctx:
        def sb(name, shape, dt=F32):
            return ctx.enter_context(nc.sbuf_tensor(name, shape, dt))

        def sem(name):
            return ctx.enter_context(nc.semaphore(name))

        def pair(name):
            return [sem(name + "_even"), sem(name + "_odd")]

        def steps(name, names):
            return Steps(sem(name), names)

        def signals(prefix, names):
            return {n: steps(f"{prefix}_{n}", n) for n in names.split()}

        T1 = nc.dram_tensor("T1", (2 * N, C), F32, kind="Internal").ap()
        T2 = nc.dram_tensor("T2", (2 * N, C), F32, kind="Internal").ap()
        restart_d = nc.dram_tensor("restart_d", (TILES * P,), BF16, kind="Internal").ap()
        T1n = T1.rearrange("(n two) c -> n (two c)", two=2)
        T2n = T2.rearrange("(n two) c -> n (two c)", two=2)

        ident = sb("ident", [P, P])
        zero = sb("zero", [P, C])
        Wk = [sb(f"Wk{i}", [P, KC, K, C]) for i in (1, 2)]
        root = [sb(f"rootpair{i}", [P, P]) for i in (1, 2)]
        bias = [sb(f"bias{i}r", [P, C]) for i in (1, 2)]
        Wd1 = sb("Wd1blocks", [4 * MT, MT, C])
        Wd2 = sb("Wd2blocks", [P, 2, C])
        bd2 = sb("bd2r", [P, 1, C])
        mcol = {n: sb(f"{n}c", [P, 1]) for n in ("g1", "b1", "g2", "b2")}
        wsum = sb("wsum", [P, 2, MT])
        spread = sb("spread", [P, 2, P])
        Wqk = sb("Wqk", [P, 2, C])
        Wv = sb("Wv", [P, 2, C])

        srcI = sb("srcI", [P, TILES], I32)
        dstI = sb("dstI", [P, TILES], I32)
        halfI = sb("halfI", [P, TILES], I32)
        outI = sb("outI", [P, TILES], I32)
        A01 = sb("A01", [P, 2, TILES, K])
        A0, A1 = A01[:, 0], A01[:, 1]
        E3x = sb("E3x", [P, MG * MT, 4])
        DT = sb("DT", [P, MG * MT // 2, P])
        restart = sb("restart", [P, TILES * P], BF16)

        arena = sb("arena", [P, ARENA])

        class Arena:
            def __init__(self, start=0):
                self.at = start

            def take(self, shape, dt=F32):
                n = 1
                for d in shape[1:]:
                    n *= d
                words = n // 2 if dt == BF16 else n
                v = arena[0:shape[0], self.at:self.at + words]
                self.at += words
                assert self.at <= ARENA
                if dt != F32:
                    v = v.bitcast(dt)
                if len(shape) == 2:
                    return v
                if len(shape) == 3:
                    return v.rearrange("p (a b) -> p a b", a=shape[1])
                return v.rearrange("p (a b c) -> p a b c", a=shape[1], b=shape[2])

        first = Arena()
        rows_i = first.take([P, 4, 2 * P], I32)
        rows_f = first.take([P, 4, 2 * P])
        rows_r = first.take([P, 2 * P], BF16)
        ends_r = first.take([P, 2 * P])
        begins_r = first.take([P, 2 * P])
        ea2 = first.take([P, 2, P * 2])
        ea3 = first.take([P, 2, P * 3])

        vcol = sb("vcol", [P, 2, TILES])
        knots = sb("knots", [P, K + 1])

        mc = DT.rearrange("p t e -> p (t e)").rearrange("p (t c) -> p t c", c=C)
        mst = sb("mst", [P, 3, MG * MT])
        e3s = [sb(f"e3s{i}", [P, MT * 4]) for i in (0, 1)]

        gath = [sb(f"gath{i}", [P, TPG, 2, 2 * C]) for i in (0, 1)]
        gidx = [sb(f"gidx{i}", [P, 2 * TPG], I32) for i in (0, 1)]
        sidx = [sb(f"sidx{i}", [P, TPG], I32) for i in (0, 1)]
        srow = [sb(f"srow{i}", [P, TPG, C]) for i in (0, 1)]
        lnc = sb("lnc", [P, 2 * TPG, C])
        lnq = sb("lnq", [P, 2 * TPG, C])
        lns = sb("lns", [P, 8, 2 * TPG])
        a0r = sb("a0r", [P, TPG, K])
        jst = sb("jst", [P, 5, TPG + NPP])

        msg = sb("msg", [P, TPG, C])
        nhT = sb("nhT", [P, 4 * P])
        nst = sb("nst", [P, 4, NPP])
        conv_mem = Arena()
        nx = [conv_mem.take([P, NPP, C]) for _ in (0, 1)]
        nt = [conv_mem.take([P, NPP, 2 * C]) for _ in (0, 1)]
        no = [conv_mem.take([P, NPP, C]) for _ in (0, 1)]
        nln, nq, nh = (conv_mem.take([P, NPP, C]) for _ in range(3))
        mlp_mem = Arena(conv_mem.at)
        V = conv_mem.take([P, TPG, K * C])
        ZT = [conv_mem.take([P, KC, P]) for _ in (0, 1)]
        Z = [conv_mem.take([P, TPG, KC * P]) for _ in (0, 1)]
        agg = [conv_mem.take([C, EG]) for _ in (0, 1)]
        mx = [mlp_mem.take([P, MT * C]) for _ in (0, 1)]
        mg = [mlp_mem.take([P, MT * C]) for _ in (0, 1)]
        mq = [lnc, lnq]
        e3T = [nhT[0:4 * MT, i * P:i * P + P] for i in (0, 1)]
        att_mem = Arena()
        x1 = [att_mem.take([P, 2 * TPG, C]) for _ in (0, 1)]
        xn = att_mem.take([P, TPG, 2 * C])
        pp, d0, lm, dm = (att_mem.take([P, EG]) for _ in range(4))
        mb = [att_mem.take([P, EG + 1]) for _ in (0, 1)]
        sums = [att_mem.take([P, EG]) for _ in (0, 1)]
        rec = att_mem.take([P, TPG, C])
        XT = [att_mem.take([P, EG]) for _ in (0, 1)]
        mx3 = [att_mem.take([P, MT * C]) for _ in (0, 1)]

        turns = []
        for b, width in ((0, P), (1, ROWS1)):
            cols = slice(b * P, b * P + width)
            for q, t in ((0, srcI), (1, dstI), (2, outI), (3, halfI)):
                turns.append((rows_f[:, q, b * P:b * P + P], t[:, cols]))
            for c in (0, 1):
                turns.append((ea2[:, b, :].rearrange("t (p c) -> t c p", c=2)[:, c], vcol[:, c, cols]))
            for c in (0, 1, 2):
                turns.append((ea3[:, b, :].rearrange("t (p c) -> t c p", c=3)[:, c], E3x[:, cols, c]))
        PREP = 7
        COLS = len(turns)
        ROW_LOADS = 16 * 19
        MLP_WEIGHTS = 16 * (2 + 1 + 2 * len(mcol))
        WEIGHTS = 16 * (2 * (K + 3) + 6)

        bank = [ctx.enter_context(nc.psum_tensor(f"bank{i}", [P, 512], F32)) for i in range(8)]

        s_mem = sem("memsets")
        s_rows = sem("rows_loaded")
        s_w1 = sem("Wd1_loaded")
        s_mw = sem("mlp_weights_loaded")
        s_w = sem("weights_loaded")
        s_id = sem("ident_built")
        s_prep = sem("rows_prepared")
        s_tr = sem("rows_turned")
        s_col = sem("columns_stored")
        s_hat = sem("hats_made")
        s_neg = sem("W2_negated")
        s_wc = sem("weights_centred")
        s_rst = sem("restarts_written")
        s_rsb = sem("restarts_spread")
        s_zero = {1: sem("T1_zeroed"), 2: sem("T2_zeroed")}
        pool_gate, pe_gate, sp_gate = sem("pool_gate"), sem("pe_gate"), sem("sp_gate")

        block = ctx.enter_context(nc.Block())

        def each(eng, step, before, after, n=G, ahead=2, first=0):
            middle = first + 3
            rounds = max(0, (n - ahead - middle) // UNROLL)
            for g in range(first - before, middle):
                step(Group(None, g))
            if rounds:
                with eng.Fori(0, rounds) as h:
                    for g in range(middle, middle + UNROLL):
                        step(Group(h, g))
            for g in range(middle + UNROLL * rounds, n + after):
                step(Group(None, g))

        def tiles_of(t, g):
            return t[:, bass.ds(g.times(TPG), TPG)]

        def half_of(g):
            return slice(g.parity * TPG, g.parity * TPG + TPG)

        m1 = signals("mlp1", "copy turn turned product square keep var")
        m2 = signals("mlp2", "norm turn gelu product keep square var")
        m3 = signals("mlp3", "norm turn gelu")
        s_mvar, s_mroot = sem("mlp_variances"), sem("mlp_roots")

        def end_of(eng, steps_, n=G):
            eng.wait_ge(steps_.sem, n * len(steps_.names))

        NEWTON = "seed " + " ".join(f"n{i}{c}" for i in range(3) for c in "abc")

        def conv_sems(n):
            s = {
                "gathered": pair(f"c{n}_gathered"), "scattered": pair(f"c{n}_scattered"),
                "nload": pair(f"c{n}_nload"), "nstore": pair(f"c{n}_nstore"),
                "z": steps(f"c{n}_z", "z0 z1 z2 z3"), "turn": steps(f"c{n}_turn", "t0 t1 t2 t3"), "prod": steps(f"c{n}_prod", "m0 m1 m2 m3"),
                "zt": steps(f"c{n}_zt", "zt0 zt1 zt2 zt3"), "comb": steps(f"c{n}_comb", "v0 v1 v2 half v3 msg"),
                "npe": steps(f"c{n}_npe", "nt nr"), "out": steps(f"c{n}_out", "out" if n == 1 else "acc out"),
                **signals(f"c{n}", "gidx sidx mt agg at row xn nts"),
            }
            if n == 1:
                s.update(signals("c1", "esum ecen esq evar nsum ncen nsq nvar root a0r"))
                s["norm"] = steps("c1_norm", "mean eps rstd")
            else:
                s.update(signals("c2", "h"))
            return s

        cs = {1: conv_sems(1), 2: conv_sems(2)}
        at = {
            "gathered": pair("a_gathered"), "scattered": pair("a_scattered"),
            "gidx": steps("a_gidx", "src dst"), "x1": steps("a_x1", "dst src"),
            "norm": steps("a_norm", "mean eps " + NEWTON), "q": steps("a_q", "q1 q2"),
            "s1": steps("a_s1", "carry max lm step cut"), "exp": steps("a_exp", "p d0"),
            "s2": steps("a_s2", "pv scan"), "fin": steps("a_fin", "rec y out"),
            **signals("a", "sidx sum cen sq var xn xt xts rt"),
        }

        def scatter_done(eng, s):
            for par in (0, 1):
                eng.wait_ge(s["scattered"][par], 16 * TPG * ((G + 1 - par) // 2))

        def node_stores_done(eng, s, per):
            for par in (0, 1):
                eng.wait_ge(s["nstore"][par], per * ((G + 1 - par) // 2))

        @block.sync
        def _(sp):
            sp.wait_ge(s_mem, 5)
            for q, name in ((0, "src"), (1, "dst")):
                v = a[name]
                sp.dma_start(rows_i[:, q, 0:P], v[0:P * P].rearrange("(t p) -> t p", p=P)).then_inc(s_rows, 16)
                sp.dma_start(rows_i[0:FULL1, q, P:2 * P],
                             v[P * P:P * P + FULL1 * P].rearrange("(t p) -> t p", p=P)).then_inc(s_rows, 16)
                sp.dma_start(rows_i[FULL1:FULL1 + 1, q, P:P + REST],
                             v[E - REST:E].rearrange("(t p) -> t p", t=1)).then_inc(s_rows, 16)
            dst = a["dst"]
            sp.dma_start(rows_i[0:1, 2, 1:P], dst[0:P - 1].rearrange("(t p) -> t p", t=1)).then_inc(s_rows, 16)
            sp.dma_start(rows_i[1:P, 2, 0:P], dst[P - 1:P * P - 1].rearrange("(t p) -> t p", p=P)).then_inc(s_rows, 16)
            sp.dma_start(rows_i[0:FULL1, 2, P:2 * P],
                         dst[P * P - 1:P * P - 1 + FULL1 * P].rearrange("(t p) -> t p", p=P)).then_inc(s_rows, 16)
            sp.dma_start(rows_i[FULL1:FULL1 + 1, 2, P:P + REST],
                         dst[E - REST - 1:E - 1].rearrange("(t p) -> t p", t=1)).then_inc(s_rows, 16)
            sp.dma_start(rows_i[:, 3, 0:P], dst[1:P * P + 1].rearrange("(t p) -> t p", p=P)).then_inc(s_rows, 16)
            sp.dma_start(rows_i[0:FULL1, 3, P:2 * P],
                         dst[P * P + 1:P * P + 1 + FULL1 * P].rearrange("(t p) -> t p", p=P)).then_inc(s_rows, 16)
            sp.dma_start(rows_i[FULL1:FULL1 + 1, 3, P:P + REST - 1],
                         dst[E - REST + 1:E].rearrange("(t p) -> t p", t=1)).then_inc(s_rows, 16)
            for buf, name in ((ea2, "edge_attr_2"), (ea3, "edge_attr_3")):
                v = a[name]
                sp.dma_start(buf[:, 0], v[0:P * P, :].rearrange("(t p) c -> t (p c)", p=P)).then_inc(s_rows, 16)
                sp.dma_start(buf[0:FULL1, 1], v[P * P:P * P + FULL1 * P, :].rearrange("(t p) c -> t (p c)", p=P))\
                    .then_inc(s_rows, 16)
                sp.dma_start(buf[FULL1:FULL1 + 1, 1, 0:REST * v.shape[1]],
                             v[E - REST:E, :].rearrange("(t p) c -> t (p c)", t=1)).then_inc(s_rows, 16)
            sp.wait_ge(s_prep, PREP)
            sp.dma_start(restart_d[0:P * P].rearrange("(t p) -> t p", p=P), rows_r[:, 0:P]).then_inc(s_rst, 16)
            sp.dma_start(restart_d[P * P:TILES * P].rearrange("(t p) -> t p", p=P),
                         rows_r[0:ROWS1, P:2 * P]).then_inc(s_rst, 16)
            sp.wait_ge(s_rst, 32)
            sp.wait_ge(s_mw, MLP_WEIGHTS)
            sp.dma_start(restart[:, :], restart_d.rearrange("(a e) -> a e", a=1).broadcast_to([P, TILES * P]))\
                .then_inc(s_rsb, 16)

            sp.wait_ge(s_w, WEIGHTS)
            ZP = 80
            sp.dma_start(T1.rearrange("(p r two) c -> two p r c", p=ZP, two=2)[1],
                         zero[0:ZP, :].unsqueeze(1).broadcast_to([ZP, N // ZP, C])).then_inc(s_zero[1], 16)

            def node_rows(view, g):
                if g.h is None and g.off == NGROUPS - 1:
                    return view[(NGROUPS - 1) * NG:N].rearrange("(p j) c -> p j c", j=NPP), TAILP
                return view[bass.ds(g.times(NG), NG)].rearrange("(p j) c -> p j c", j=NPP), P

            sp.wait_ge(s_col, COLS)
            s = cs[1]

            def step1(g):
                if (g + 2).within(G):
                    n = g + 2
                    wait(sp, s["ncen"], n - 2)
                    sp.sem_inc(sp_gate, 1)
                    rows, p = node_rows(a["x"], n)
                    sp.dma_start(nx[n.parity][0:p], rows).then_inc(s["nload"][n.parity], 16)
                if g.within(G):
                    rows, p = node_rows(T2n, g)
                    sp.dma_start(rows[:, :, C:2 * C], zero[0:p, :].unsqueeze(1).broadcast_to([p, NPP, C]))\
                        .then_inc(s_zero[2], 16)
                    wait(sp, s["out"], g, "out")
                    sp.sem_inc(sp_gate, 1)
                    rows, p = node_rows(T1n, g)
                    sp.dma_start(rows[:, :, 0:C], no[g.parity][0:p]).then_inc(s["nstore"][g.parity], 16)

            each(sp, step1, 2, 0, ahead=3)

            t = cs[2]
            scatter_done(sp, s)
            node_stores_done(sp, s, 16)

            def step2(g):
                if (g + 1).within(G):
                    n = g + 1
                    wait(sp, t["xn"], n - 2)
                    sp.sem_inc(sp_gate, 1)
                    wait(sp, t["out"], n - 2, "acc")
                    sp.sem_inc(sp_gate, 1)
                    rows, p = node_rows(T1n, n)
                    sp.dma_start(nt[n.parity][0:p], rows).then_inc(t["nload"][n.parity], 16)
                    rows, p = node_rows(a["x"], n)
                    sp.dma_start(nx[n.parity][0:p], rows).then_inc(t["nload"][n.parity], 16)
                if (g - 1).within(G):
                    n = g - 1
                    wait(sp, t["out"], n, "out")
                    sp.sem_inc(sp_gate, 1)
                    rows, p = node_rows(T2n, n)
                    sp.dma_start(rows[:, :, 0:C], no[n.parity][0:p]).then_inc(t["nstore"][n.parity], 16)
                    rows, p = node_rows(out, n)
                    sp.dma_start(rows, no[n.parity][0:p]).then_inc(t["nstore"][n.parity], 16)

            each(sp, step2, 1, 1)

        @block.gpsimd
        def _(pool):
            pool.memset(ident[:, :], 0.0).then_inc(s_id, 1)
            pool.wait_ge(s_id, 1)
            pool.affine_select(out=ident[:, :], in_=ident[:, :], compare_op=ALU.not_equal, fill=1.0, base=0,
                               pattern=[[-1, P]], channel_multiplier=1).then_inc(s_id, 1)
            pool.wait_ge(s_mem, 7)
            for i in (0, 1):
                W = a[f"L0_gnn_W{i + 1}"]
                for k0 in range(K):
                    lo = C * (k0 % 2)
                    pool.dma_start(Wk[i][lo:lo + C, k0 // 2],
                                  W.rearrange("(k1 k0) i o -> k0 i k1 o", k0=K)[k0]).then_inc(s_w, 16)
                for q in (0, 1):
                    pool.dma_start(root[i][C * q:C * q + C, C * q:C * q + C], a[f"L0_gnn_root{i + 1}"])\
                        .then_inc(s_w, 16)
                pool.dma_start(bias[i][:, :], a[f"L0_gnn_bias{i + 1}"].rearrange("(a c) -> a c", a=1)
                              .broadcast_to([P, C])).then_inc(s_w, 16)
            for q in (0, 1):
                pool.dma_start(Wqk[0:C, q, :], a["L1_gnn_W1"]).then_inc(s_w, 16)
                pool.dma_start(Wqk[C:P, q, :], a["L1_gnn_W2"]).then_inc(s_w, 16)
                pool.dma_start(Wv[C:P, q, :], a["L1_gnn_W3"]).then_inc(s_w, 16)
            half_bound = pool.to_reg(2 * N - 1)
            out_bound = pool.to_reg(N - 1)

            def gather(g, s, table, width, sets):
                for k in range(sets):
                    for j in range(TPG):
                        pool.indirect_dma_start(
                            out=gath[g.parity][:, j, k, 0:width], out_offset=None, in_=table,
                            in_offset=bass.IndirectOffsetOnAxis(gidx[g.parity][:, k * TPG + j:k * TPG + j + 1], 0),
                        ).then_inc(s["gathered"][g.parity], 16)

            def scatter(g, s, table, bound):
                for j in range(TPG):
                    pool.indirect_dma_start(
                        out=table,
                        out_offset=bass.IndirectOffsetOnAxis(sidx[g.parity][:, j:j + 1], 0),
                        in_=srow[g.parity][:, j, :], in_offset=None, bounds_check=bound, oob_is_err=False,
                    ).then_inc(s["scattered"][g.parity], 16)

            def conv(s, table, width, target, zeroed, read, ahead):
                def step(g):
                    if (g + ahead).within(G):
                        n = g + ahead
                        wait(pool, s["gidx"], n)
                        wait(pool, s[read], n - 2)
                        pool.sem_inc(pool_gate, 1)
                        gather(n, s, table, width, 1)
                    if (g - 1).within(G):
                        n = g - 1
                        if n.h is None and n.off == 0:
                            pool.wait_ge(*zeroed)
                        wait(pool, s["sidx"], n)
                        wait(pool, s["row"], n)
                        pool.sem_inc(pool_gate, 1)
                        scatter(n, s, target, half_bound)

                each(pool, step, ahead, 1, ahead=ahead)

            conv(cs[1], a["x"], C, T1, (s_zero[1], 16), "ecen", 3)
            scatter_done(pool, cs[1])
            node_stores_done(pool, cs[1], 16)
            conv(cs[2], T1n, 2 * C, T2, (s_zero[2], 16 * G), "h", 2)
            scatter_done(pool, cs[2])
            node_stores_done(pool, cs[2], 32)

            def step(g):
                if (g + 3).within(G):
                    n = g + 3
                    wait(pool, at["gidx"], n, "dst")
                    wait(pool, at["x1"], n - 2, "src")
                    pool.sem_inc(pool_gate, 1)
                    gather(n, at, T2n, 2 * C, 2)
                if (g - 1).within(G):
                    n = g - 1
                    wait(pool, at["sidx"], n)
                    wait(pool, at["fin"], n, "out")
                    pool.sem_inc(pool_gate, 1)
                    scatter(n, at, out, out_bound)

            each(pool, step, 3, 1, ahead=3)
            scatter_done(pool, at)

        @block.scalar
        def _(act):
            act.wait_ge(s_mem, 7)
            for j in range(MT):
                act.dma_start(Wd1[4 * j:4 * j + 3, j, :], a["L1_gnn_Wd1"]).then_inc(s_w1, 16)
                act.dma_start(Wd1[4 * j + 3:4 * j + 4, j, :], a["L1_gnn_bd1"].rearrange("(a c) -> a c", a=1))\
                    .then_inc(s_w1, 16)
            for q in (0, 1):
                act.dma_start(Wd2[C * q:C * q + C, q, :], a["L1_gnn_Wd2"]).then_inc(s_mw, 16)
                for n, t in mcol.items():
                    act.dma_start(t[C * q:C * q + C, :], a[f"L1_gnn_{n}"].rearrange("(c a) -> c a", a=1))\
                        .then_inc(s_mw, 16)
            act.dma_start(bd2[:, 0, :], a["L1_gnn_bd2"].rearrange("(a c) -> a c", a=1).broadcast_to([P, C]))\
                .then_inc(s_mw, 16)
            def conv_gidx(s, g):
                wait_fill(act, s["gathered"], g - 2, 16 * TPG)
                act.activation(gidx[g.parity][:, 0:TPG], tiles_of(srcI, g), ACT.Copy).then_inc(s["gidx"].sem, 1)

            def hat_weights():
                for k in range(K):
                    act.activation(A01[:, :, :, k], vcol[:, :, :], ACT.Abs, scale=float(K - 1), bias=knots[:, k:k + 1])\
                        .then_inc(s_hat, 1)
                for k in range(K):
                    act.wait_ge(s_hat, K)
                    act.activation(A01[:, :, :, k], A01[:, :, :, k], ACT.Relu, scale=-1.0, bias=knots[:, K:K + 1])\
                        .then_inc(s_hat, 1)

            act.wait_ge(s_col, COLS)
            for g in (0, 1):
                conv_gidx(cs[1], Group(None, g))

            def step(g):
                if (g + 2).within(MG):
                    e = g + 2
                    wait(act, m1["turn"], e - 2)
                    act.activation(e3s[e.parity][:, :].rearrange("p (t c) -> p t c", c=4),
                                   E3x[:, bass.ds(e.times(MT), MT), :], ACT.Copy).then_inc(m1["copy"].sem, 1)
                if (g + 1).within(MG):
                    e = g + 1
                    wait(act, m1["turn"], e)
                    wait(act, m1["product"], e - 2)
                    act.activation(e3T[e.parity], bank[e.parity][0:4 * MT, 0:P], ACT.Copy)\
                        .then_inc(m1["turned"].sem, 1)
                if g.h is None and g.off == 0:
                    hat_weights()
                if (g - 1).within(MG):
                    e = g - 1
                    wait(act, m1["keep"], e)
                    wait(act, m1["var"], e - 2)
                    act.activation(mq[e.parity][:, :, :], mc[:, bass.ds(e.times(MT), MT), :], ACT.Square)\
                        .then_inc(m1["square"].sem, 1)

            each(act, step, 2, 1, MG)
            act.wait_ge(s_mvar, 1)
            act.activation(mst[:, 2, :], mst[:, 1, :], ACT.Sqrt).then_inc(s_mroot, 1)

            def layer2(first, last):
                def step(g):
                    if (g + 1).within(last, first):
                        e = g + 1
                        wait(act, m2["turn"], e)
                        wait(act, m2["product"], e - 2)
                        act.activation(mg[e.parity], bank[e.parity][:, :], ACT.Gelu, scale=mcol["g1"][:, :],
                                       bias=mcol["b1"][:, :]).then_inc(m2["gelu"].sem, 1)
                    if g.within(last, first):
                        wait(act, m2["keep"], g)
                        wait(act, m2["var"], g - 2)
                        act.activation(mq[g.parity][:, :, :], mc[:, bass.ds(g.times(MT), MT), :], ACT.Square)\
                            .then_inc(m2["square"].sem, 1)

                each(act, step, 1, 0, last, first=first)

            layer2(*LAYER2[0])
            def conv(n):
                s = cs[n]
                ahead = 3 if n == 1 else 2

                def step(g):
                    def evacuate(g, j):
                        wait(act, s["turn"], g, f"t{j}")
                        act.activation(ZT[j % 2][:, :, :], bank[j % 2][:, 0:KC * P], ACT.Relu)\
                            .then_inc(s["zt"].sem, 1)

                    if (g + ahead).within(G, 2):
                        conv_gidx(s, g + ahead)
                    if (g - 1).within(G):
                        e = g - 1
                        wait_fill(act, s["scattered"], e - 2, 16 * TPG)
                        act.activation(sidx[e.parity][:, :], tiles_of(halfI, e), ACT.Copy)\
                            .then_inc(s["sidx"].sem, 1)
                    if g.within(G):
                        evacuate(g, 2)
                    if n == 1 and (g + 2).within(G):
                        wait(act, s["ecen"], g + 2)
                        wait(act, s["evar"], g + 1)
                        act.activation(lnq[:, 0:TPG, :], lnc[:, half_of(g), :], ACT.Square)\
                            .then_inc(s["esq"].sem, 1)
                    if n == 1 and (g + 1).within(G):
                        wait(act, s["ncen"], g + 1)
                        wait(act, s["nvar"], g)
                        act.activation(nq[:, :, :], nln[:, :, :], ACT.Square).then_inc(s["nsq"].sem, 1)
                    if g.within(G):
                        wait(act, s["npe"], g, "nt")
                        act.activation(nhT[:, :], bank[6][:, :], ACT.Relu).then_inc(s["nts"].sem, 1)
                        evacuate(g, 3)
                    if n == 1 and ((g + 1).within(G) or (g + 2).within(G)):
                        wait(act, s["norm"], g + 2, "eps")
                        act.activation(jst[:, 4, :], jst[:, 2, :], ACT.Sqrt).then_inc(s["root"].sem, 1)
                    if (g + 1).within(G):
                        evacuate(g + 1, 0)
                        evacuate(g + 1, 1)
                    if (g - 1).within(G):
                        e = g - 1
                        wait(act, s["at"], e)
                        act.activation(srow[e.parity][:, :, :], bank[5][:, 0:TPG * C], ACT.Copy)\
                            .then_inc(s["row"].sem, 1)

                each(act, step, ahead, 1, ahead=ahead)

            act.wait_ge(s_w, WEIGHTS)
            nc.scalar.mul(Wqk[C:P, :, :], Wqk[C:P, :, :], -1.0).then_inc(s_neg, 1)

            conv(1)
            for g in (0, 1):
                wait_fill(act, cs[1]["gathered"], Group(None, G - 2 + g), 16 * TPG)
                conv_gidx(cs[2], Group(None, g))
            layer2(*LAYER2[1])
            conv(2)

            def copy_gidx(g):
                wait_fill(act, at["gathered"], g - 2, 32 * TPG)
                for k, t in ((0, srcI), (1, dstI)):
                    act.activation(gidx[g.parity][:, k * TPG:(k + 1) * TPG], tiles_of(t, g), ACT.Copy)\
                        .then_inc(at["gidx"].sem, 1)

            for g in (0, 1):
                wait_fill(act, cs[2]["gathered"], Group(None, G - 2 + g), 16 * TPG)
                copy_gidx(Group(None, g))

            act.wait_ge(s_mvar, 2)
            act.activation(mst[:, 2, :], mst[:, 1, :], ACT.Sqrt).then_inc(s_mroot, 1)

            def step(g):
                wait(act, m3["turn"], g)
                act.activation(DT[:, bass.ds(g.times(MT // 2), MT // 2), :],
                               bank[g.parity][:, :].rearrange("p (t e) -> p t e", e=P), ACT.Gelu,
                               scale=mcol["g2"][:, :], bias=mcol["b2"][:, :]).then_inc(m3["gelu"].sem, 1)

            each(act, step, 0, 0, MG)


            def step(g):
                if (g - 1).within(G):
                    e = g - 1
                    wait_fill(act, at["scattered"], e - 2, 16 * TPG)
                    act.activation(sidx[e.parity][:, :], tiles_of(outI, e), ACT.Copy).then_inc(at["sidx"].sem, 1)
                if (g + 1).within(G):
                    wait(act, at["cen"], g + 1)
                    wait(act, at["var"], g)
                    act.activation(lnq[:, :, :], lnc[:, :, :], ACT.Square).then_inc(at["sq"].sem, 1)
                if (g + 3).within(G, 2):
                    copy_gidx(g + 3)
                if g.within(G):
                    wait(act, at["s1"], g, "lm")
                    wait(act, at["s2"], g - 1, "scan")
                    act.activation(pp[:, :], lm[:, :], ACT.Exp).then_inc(at["exp"].sem, 1)
                    wait(act, at["s1"], g, "cut")
                    act.activation(d0[:, :], dm[:, :], ACT.Exp).then_inc(at["exp"].sem, 1)
                if (g + 1).within(G):
                    e = g + 1
                    wait(act, at["xt"], e)
                    wait(act, at["q"], e - 2, "q2")
                    act.activation(XT[e.parity][:, :], bank[e.parity][:, :], ACT.Relu).then_inc(at["xts"].sem, 1)

            each(act, step, 3, 1, ahead=3)

        @block.tensor
        def _(pe):
            pe.wait_ge(s_id, 2)
            pe.wait_ge(s_prep, PREP)
            for n, (v, _) in enumerate(turns):
                if n >= 8:
                    pe.wait_ge(s_col, n - 7)
                pe.transpose(bank[n % 8][:, 0:P], v, ident[:, :]).then_inc(s_tr, 1)
            pe.wait_ge(s_col, COLS)

            pe.wait_ge(s_wc, 3)

            def step(g):
                if (g + 1).within(MG):
                    e = g + 1
                    wait(pe, m1["copy"], e)
                    wait(pe, m1["turned"], e - 2)
                    pe.sem_inc(pe_gate, 1)
                    pe.transpose(bank[e.parity][0:4 * MT, 0:P], e3s[e.parity][:, :], ident[:, :])\
                        .then_inc(m1["turn"].sem, 1)
                if g.within(MG):
                    wait(pe, m1["turned"], g)
                    wait(pe, m1["keep"], g - 2)
                    pe.sem_inc(pe_gate, 1)
                    pe.matmul(bank[2 + g.parity][:, :], e3T[g.parity], Wd1[:, :, :].rearrange("k t c -> k (t c)"),
                              start=True, stop=True).then_inc(m1["product"].sem, 1)

            each(pe, step, 1, 0, MG)

            def turn_chunk(g, s, mx):
                wait(pe, s["norm"], g)
                wait(pe, s["gelu"], g - 2)
                for q in range(MT // 2):
                    tr = pe.transpose(bank[g.parity][:, q * P:q * P + P], mx[g.parity][:, q * P:q * P + P],
                                      ident[:, :])
                tr.then_inc(s["turn"].sem, 1)

            def layer2(first, last):
                def step(g):
                    if (g + 1).within(last, first):
                        turn_chunk(g + 1, m2, mx)
                    if g.within(last, first):
                        wait(pe, m2["gelu"], g)
                        wait(pe, m2["keep"], g - 2)
                        for q in range(MT // 2):
                            mm = pe.matmul(bank[2 + g.parity][:, q * P:q * P + P], mg[g.parity][:, q * P:q * P + P],
                                           Wd2[:, :, :].rearrange("k t c -> k (t c)"), start=True, stop=True)
                        mm.then_inc(m2["product"].sem, 1)

                each(pe, step, 1, 0, last, first=first)

            pe.wait_ge(s_wc, 9)
            layer2(*LAYER2[0])

            def conv(n):
                s = cs[n]

                def turn_z(g, j):
                    wait(pe, s["z"], g, f"z{j}")
                    if j < 2:
                        wait(pe, s["zt"], g - 1, f"zt{j + 2}")
                    else:
                        wait(pe, s["zt"], g, f"zt{j - 2}")
                    for c in range(KC):
                        tr = pe.transpose(bank[j % 2][:, c * P:c * P + P], Z[g.parity][:, j, c * P:c * P + P],
                                          ident[:, :])
                    tr.then_inc(s["turn"].sem, 1)

                def product(g, j):
                    wait(pe, s["zt"], g, f"zt{j}")
                    if j < 2:
                        wait(pe, s["comb"], g - 1, f"v{j + 2}")
                    else:
                        wait(pe, s["comb"], g, f"v{j - 2}")
                    for c in range(KC):
                        mm = pe.matmul(bank[2 + j % 2][:, 0:KO], ZT[j % 2][:, c, :],
                                       Wk[n - 1][:, c].rearrange("p k o -> p (k o)"),
                                       start=(c == 0), stop=(c == KC - 1))
                    mm.then_inc(s["prod"].sem, 1)

                def step(g):
                    if g.within(G):
                        product(g, 0)
                    if (g - 1).within(G):
                        e = g - 1
                        wait(pe, s["comb"], e, "msg")
                        wait(pe, s["agg"], e - 1)
                        pe.sem_inc(pe_gate, 1)
                        for j in range(TPG):
                            tr = pe.transpose(bank[4][0:C, j * P:j * P + P], msg[:, j, :], ident[:, :])
                        tr.then_inc(s["mt"].sem, 1)
                    if g.within(G):
                        turn_z(g, 2)
                        product(g, 1)
                        wait(pe, s["xn"], g)
                        wait(pe, s["nts"], g - 1)
                        pe.sem_inc(pe_gate, 1)
                        for q in range(4):
                            tr = pe.transpose(bank[6][:, q * P:q * P + P],
                                              nh[:, 2 * q:2 * q + 2, :].rearrange("p t c -> p (t c)"), ident[:, :])
                        tr.then_inc(s["npe"].sem, 1)
                        turn_z(g, 3)
                        product(g, 2)
                    if (g + 1).within(G):
                        turn_z(g + 1, 0)
                    if g.within(G):
                        wait(pe, s["nts"], g)
                        wait(pe, s["out"], g - 1, "out" if n == 1 else "acc")
                        for q in range(4):
                            mm = pe.matmul(bank[7][:, q * P:q * P + P], nhT[:, q * P:q * P + P], root[n - 1][:, :],
                                           start=True, stop=True)
                        mm.then_inc(s["npe"].sem, 1)
                        product(g, 3)
                    if (g + 1).within(G):
                        turn_z(g + 1, 1)
                    if (g - 1).within(G):
                        e = g - 1
                        wait(pe, s["agg"], e)
                        wait(pe, s["row"], e - 1)
                        pe.sem_inc(pe_gate, 1)
                        for j in range(TPG):
                            tr = pe.transpose(bank[5][:, j * C:j * C + C], agg[e.parity][:, j * P:j * P + P],
                                              ident[0:C, 0:C])
                        tr.then_inc(s["at"].sem, 1)

                each(pe, step, 1, 1)

            pe.wait_ge(s_w, WEIGHTS)
            pe.wait_ge(s_neg, 1)
            conv(1)
            layer2(*LAYER2[1])
            conv(2)

            each(pe, lambda g: turn_chunk(g, m3, mx3), 0, 0, MG)
            end_of(pe, m3["gelu"], MG)

            def step(g):
                if g.within(G):
                    wait(pe, at["s2"], g, "scan")
                    wait(pe, at["fin"], g - 2, "y")
                    for j in range(TPG):
                        tr = pe.transpose(bank[6 + g.parity][:, j * P:j * P + P], sums[g.parity][:, j * P:j * P + P],
                                          ident[:, :])
                    tr.then_inc(at["rt"].sem, 1)
                if (g + 1).within(G):
                    e = g + 1
                    pairs = DT[:, bass.ds(e.times(TPG // 2), TPG // 2), :]
                    products = ((2, Wqk, "s1", "step"), (4, Wv, "s2", "pv"))
                    for b, _, reader, name in products:
                        wait(pe, at[reader], e - 2, name)
                        for j in (0, 1):
                            pe.matmul(bank[b + e.parity].rearrange("p (t h e) -> p h t e", h=2, e=P)[:, j],
                                      spread[:, j, :], pairs, start=(j == 0), stop=False, skip_group_check=True)
                    wait(pe, at["xn"], e)
                    wait(pe, at["xts"], e - 2)
                    pe.sem_inc(pe_gate, 1)
                    for j in range(TPG):
                        tr = pe.transpose(bank[e.parity][:, j * P:j * P + P], xn[:, j], ident[:, :])
                    tr.then_inc(at["xt"].sem, 1)
                    wait(pe, at["xts"], e)
                    for b, W, _, _ in products:
                        pe.matmul(bank[b + e.parity][:, :], W[:, :, :].rearrange("p t c -> p (t c)"),
                                  XT[e.parity][:, :], start=False, stop=True, skip_group_check=True)\
                            .then_inc(at["q"].sem, 1)

            each(pe, step, 1, 0)

        @block.vector
        def _(dve):
            V_ = nc.vector
            V_.memset(rows_i[:, 0], 0).then_inc(s_mem, 1)
            V_.memset(rows_i[:, 1], int(SKIP)).then_inc(s_mem, 1)
            V_.memset(rows_i[:, 2:4], -1).then_inc(s_mem, 1)
            V_.memset(ea2[:, :, :], 0.0).then_inc(s_mem, 1)
            V_.memset(ea3[:, :, :], 0.0).then_inc(s_mem, 1)
            for t in (Wk[0][C:P, KC - 1], Wk[1][C:P, KC - 1], root[0][:, :], root[1][:, :],
                      Wd1[:, :, :], Wd2[:, :, :], Wv[:, :, :], spread[:, :, :]):
                V_.memset(t, 0.0)
            for k in range(K):
                V_.memset(knots[:, k:k + 1], -float(k))
            V_.memset(knots[:, K:K + 1], 1.0)
            V_.memset(E3x[:, :, :], 1.0).then_inc(s_mem, 1)
            V_.memset(zero[:, :], 0.0).then_inc(s_mem, 1)

            n = 0

            def prep(ins):
                nonlocal n
                ins.then_inc(s_prep, 1)
                n += 1

            dve.wait_ge(s_rows, ROW_LOADS)
            dve.wait_ge(s_mem, 7)
            prep(V_.tensor_copy(rows_f[:, 0], rows_i[:, 0]))
            prep(V_.tensor_scalar(rows_f[:, 1], rows_i[:, 1], float(N - 1), None, ALU.min))
            prep(V_.tensor_tensor(begins_r, rows_i[:, 1], rows_i[:, 2], ALU.not_equal))
            dve.wait_ge(s_prep, n)
            prep(V_.tensor_scalar(rows_r[:, :], begins_r, RESTART, None, ALU.mult))
            prep(V_.tensor_tensor(ends_r, rows_i[:, 1], rows_i[:, 3], ALU.is_equal))
            dve.wait_ge(s_prep, n)
            prep(V_.scalar_tensor_tensor(out=rows_f[:, 2], in0=ends_r, scalar=SKIP, in1=rows_i[:, 1],
                                         op0=ALU.mult, op1=ALU.add))
            dve.wait_ge(s_prep, n)
            prep(V_.tensor_scalar(rows_f[:, 3], rows_f[:, 2], 2.0, 1.0, ALU.mult, ALU.add))
            assert n == PREP
            for k, (_, dest) in enumerate(turns):
                dve.wait_ge(s_tr, k + 1)
                width = dest.shape[1]
                V_.tensor_copy(dest, bank[k % 8][:, 0:width]).then_inc(s_col, 1)
            dve.wait_ge(s_col, len(turns))
            dve.wait_ge(s_w1, 16 * 2 * MT)

            def centre_weights(n, w, p, b):
                total, mean = wsum[0:p, 0, 0:b], wsum[0:p, 1, 0:b]
                if n:
                    dve.wait_ge(s_wc, 3 * n)
                V_.tensor_reduce(total, w[:, :, :], AX, ALU.add).then_inc(s_wc, 1)
                dve.wait_ge(s_wc, 3 * n + 1)
                V_.tensor_scalar(mean, total, -1.0 / C, None, ALU.mult).then_inc(s_wc, 1)
                dve.wait_ge(s_wc, 3 * n + 2)
                V_.tensor_tensor(w[:, :, :], w[:, :, :], mean.unsqueeze(2).broadcast_to([p, b, C]), ALU.add)\
                    .then_inc(s_wc, 1)

            centre_weights(0, Wd1, 4 * MT, MT)

            def chunk_of(t, g):
                return t[:, bass.ds(g.times(MT), MT), :]

            def as_chunk(t):
                return t.rearrange("p (t c) -> p t c", c=C)

            def var(g, s):
                wait(dve, s["square"], g)
                V_.tensor_reduce(mst[:, 0, bass.ds(g.times(MT), MT)], mq[g.parity][:, :, :], AX, ALU.add)\
                    .then_inc(s["var"].sem, 1)

            def roots(s, n):
                end_of(dve, s["var"], MG)
                V_.tensor_scalar(mst[:, 1, :], mst[:, 0, :], 1.0 / C, EPS, ALU.mult, ALU.add).then_inc(s_mvar, 1)
                dve.wait_ge(s_mroot, n)
                V_.reciprocal(mst[:, 1, :], mst[:, 2, :]).then_inc(s_mem, 1)
                dve.wait_ge(s_mem, 9 + n)

            def norm(g, s, mx):
                wait(dve, s["turn"], g - 2)
                V_.tensor_tensor(as_chunk(mx[g.parity]), chunk_of(mc, g),
                                 mst[:, 1, bass.ds(g.times(MT), MT)].unsqueeze(2).broadcast_to([P, MT, C]),
                                 ALU.mult).then_inc(s["norm"].sem, 1)

            def set_up():
                dve.wait_ge(s_mw, MLP_WEIGHTS)
                centre_weights(1, Wd2, P, 2)
                centre_weights(2, bd2, P, 1)
                dve.wait_ge(s_id, 2)
                for q in (0, 1):
                    half = slice(q * C, q * C + C)
                    V_.tensor_copy(spread[half, q, :].rearrange("p (h c) -> p h c", h=2),
                                   ident[half, half].unsqueeze(1).broadcast_to([C, 2, C]))
                dve.wait_ge(s_rst, 32)
                V_.memset(Z[0][:, :, KO:KC * P], 0.0)
                V_.memset(Z[1][:, :, KO:KC * P], 0.0)
                V_.memset(agg[1], 0.0).then_inc(s_mem, 1)
                V_.memset(jst[:, :, :], 1.0).then_inc(s_mem, 1)
                dve.wait_ge(s_mem, 9)

            def step(g):
                if g.within(MG):
                    wait(dve, m1["product"], g)
                    V_.tensor_copy(chunk_of(mc, g), as_chunk(bank[2 + g.parity][:, :]))\
                        .then_inc(m1["keep"].sem, 1)
                if (g - 1).within(MG):
                    var(g - 1, m1)
                if g.h is None and g.off == 2:
                    set_up()

            each(dve, step, 0, 1, MG)
            roots(m1, 1)

            def layer2(first, last):
                def step(g):
                    if (g + 2).within(last, first):
                        norm(g + 2, m2, mx)
                    if g.within(last, first):
                        wait(dve, m2["product"], g)
                        V_.tensor_tensor(chunk_of(mc, g), as_chunk(bank[2 + g.parity][:, :]),
                                         bd2[:, :, :].broadcast_to([P, MT, C]), ALU.add).then_inc(m2["keep"].sem, 1)
                    if (g - 1).within(last, first):
                        var(g - 1, m2)

                each(dve, step, 2, 1, last, first=first)

            layer2(*LAYER2[0])

            dve.wait_ge(s_rsb, 16)

            def newton(sem_, g, name, v, y, t):
                names = ["eps"] + NEWTON.split()
                wait(dve, sem_, g, names[names.index(name) - 1])
                if name == "seed":
                    ins = V_.tensor_scalar(y.bitcast(I32), v.bitcast(I32), -0.5, float(0x5F3759DF), ALU.mult, ALU.add)
                elif name[2] == "a":
                    ins = V_.tensor_tensor(t, y, y, ALU.mult)
                elif name[2] == "b":
                    ins = V_.scalar_tensor_tensor(out=t, in0=t, scalar=-0.5, in1=v, op0=ALU.mult, op1=ALU.mult)
                else:
                    ins = V_.scalar_tensor_tensor(out=y, in0=t, scalar=1.5, in1=y, op0=ALU.add, op1=ALU.mult)
                ins.then_inc(sem_.sem, 1)

            def conv(n):
                s = cs[n]
                jsum, jmean, jv, jy, jt = (jst[:, k, :] for k in range(5))

                def scaled(g):
                    wait(dve, s["norm"], g, "rstd")
                    wait(dve, s["z"], g - 1, "z3")
                    V_.tensor_tensor(a0r[:, :, :], tiles_of(A0, g),
                                     jy[:, 0:TPG].unsqueeze(2).broadcast_to([P, TPG, K]), ALU.mult)\
                        .then_inc(s["a0r"].sem, 1)

                def sum_ends(g):
                    wait_fill(dve, s["gathered"], g, 16 * TPG)
                    wait(dve, s["z"], g - 2, "z3")
                    V_.tensor_tensor(lnc[:, half_of(g), :], gath[g.parity][:, :, 0, 0:C],
                                     gath[g.parity][:, :, 0, C:2 * C], ALU.add).then_inc(s["h"].sem, 1)

                def spread_z(g, j):
                    if n == 1:
                        wait(dve, s["a0r"], g)
                        w = a0r[:, j, :]
                    else:
                        wait(dve, s["h"], g)
                        w = A0[:, bass.ds(g.times(TPG, j), 1), :].rearrange("p t k -> p (t k)")
                    wait(dve, s["turn"], g - 2, f"t{j}")
                    i = g.parity * TPG + j
                    V_.tensor_tensor(Z[g.parity][:, j, 0:KO].rearrange("p (k c) -> p k c", c=C),
                                     lnc[:, i:i + 1, :].broadcast_to([P, K, C]),
                                     w.unsqueeze(2).broadcast_to([P, K, C]), ALU.mult).then_inc(s["z"].sem, 1)

                def scan(g):
                    wait(dve, s["mt"], g)
                    wait(dve, s["at"], g - 2)
                    wait(dve, s["agg"], g - 1)
                    V_.tensor_tensor_scan(agg[g.parity][:, :], restart[0:C, bass.ds(g.times(EG), EG)],
                                          bank[4][0:C, :], agg[1 - g.parity][:, EG - 1:EG], ALU.add, ALU.max)\
                        .then_inc(s["agg"].sem, 1)

                def weigh(g, j):
                    wait(dve, s["prod"], g, f"m{j}")
                    wait(dve, s["comb"], g - 1, "msg")
                    V_.tensor_tensor(V[:, j].rearrange("p (k o) -> p k o", o=C),
                                     bank[2 + j % 2][:, 0:KO].rearrange("p (k o) -> p k o", o=C),
                                     A1[:, bass.ds(g.times(TPG, j), 1), :].rearrange("p t k -> p (t k)")
                                     .unsqueeze(2).broadcast_to([P, K, C]), ALU.mult).then_inc(s["comb"].sem, 1)

                def add_knots(g, half):
                    tiles = slice(2 * half, 2 * half + 2)
                    wait(dve, s["comb"], g, ("v1", "v3")[half])
                    wait(dve, s["mt"], g - 1)
                    V_.tensor_reduce(msg[:, tiles, :], V[:, tiles].rearrange("p j (k o) -> p j o k", o=C), AX, ALU.add)\
                        .then_inc(s["comb"].sem, 1)

                def node_in(g):
                    if n == 1:
                        wait(dve, s["norm"], g + 1, "rstd")
                        wait(dve, s["npe"], g - 1, "nt")
                        V_.tensor_tensor(nh[:, :, :], nln[:, :, :],
                                         jy[:, TPG:].unsqueeze(2).broadcast_to([P, NPP, C]), ALU.mult)\
                            .then_inc(s["xn"].sem, 1)
                    else:
                        wait_fill(dve, s["nload"], g, 32)
                        wait(dve, s["npe"], g - 1, "nt")
                        V_.tensor_tensor(nh[:, :, :], nt[g.parity][:, :, 0:C], nt[g.parity][:, :, C:2 * C], ALU.add)\
                            .then_inc(s["xn"].sem, 1)

                def node_out(g):
                    wait(dve, s["npe"], g, "nr")
                    wait_fill(dve, s["nstore"], g - 2, 16 if n == 1 else 32)
                    r = bank[7][:, :].rearrange("p (t c) -> p t c", c=C)
                    o = no[g.parity][:, :, :]
                    if n == 2:
                        V_.tensor_tensor(o, r, nx[g.parity][:, :, :], ALU.add).then_inc(s["out"].sem, 1)
                        wait(dve, s["out"], g, "acc")
                        r = o
                    V_.tensor_tensor(o, r, bias[n - 1][:, :].unsqueeze(1).broadcast_to([P, NPP, C]), ALU.add)\
                        .then_inc(s["out"].sem, 1)

                def sums(g):
                    wait(dve, s["norm"], g - 1, "eps")
                    if g.within(G):
                        wait_fill(dve, s["gathered"], g, 16 * TPG)
                        V_.tensor_reduce(jsum[:, 0:TPG], gath[g.parity][:, :, 0, 0:C], AX, ALU.add)\
                            .then_inc(s["esum"].sem, 1)
                    if (g - 1).within(G):
                        wait_fill(dve, s["nload"], g - 1, 16)
                        V_.tensor_reduce(jsum[:, TPG:], nx[1 - g.parity][:, :, :], AX, ALU.add)\
                            .then_inc(s["nsum"].sem, 1)

                def mean(g):
                    if g.within(G):
                        wait(dve, s["esum"], g)
                    if (g - 1).within(G):
                        wait(dve, s["nsum"], g - 1)
                    wait(dve, s["ecen"], g - 1)
                    wait(dve, s["ncen"], g - 2)
                    V_.tensor_scalar(jmean, jsum, -1.0 / C, None, ALU.mult).then_inc(s["norm"].sem, 1)

                def centre_rows(g):
                    wait(dve, s["norm"], g, "mean")
                    if g.within(G):
                        wait(dve, s["z"], g - 2, "z3")
                        V_.tensor_tensor(lnc[:, half_of(g), :], gath[g.parity][:, :, 0, 0:C],
                                         jmean[:, 0:TPG].unsqueeze(2).broadcast_to([P, TPG, C]), ALU.add)\
                            .then_inc(s["ecen"].sem, 1)
                    if (g - 1).within(G):
                        wait(dve, s["xn"], g - 2)
                        V_.tensor_tensor(nln[:, :, :], nx[1 - g.parity][:, :, :],
                                         jmean[:, TPG:].unsqueeze(2).broadcast_to([P, NPP, C]), ALU.add)\
                            .then_inc(s["ncen"].sem, 1)

                def variances(g):
                    if g.within(G):
                        wait(dve, s["esq"], g)
                        V_.tensor_reduce(jsum[:, 0:TPG], lnq[:, 0:TPG, :], AX, ALU.add).then_inc(s["evar"].sem, 1)
                    if (g - 1).within(G):
                        wait(dve, s["nsq"], g - 1)
                        V_.tensor_reduce(jsum[:, TPG:], nq[:, :, :], AX, ALU.add).then_inc(s["nvar"].sem, 1)

                def plus_eps(g):
                    if g.within(G):
                        wait(dve, s["evar"], g)
                    if (g - 1).within(G):
                        wait(dve, s["nvar"], g - 1)
                    V_.tensor_scalar(jv, jsum, 1.0 / C, EPS, ALU.mult, ALU.add).then_inc(s["norm"].sem, 1)

                def step(g):
                    now, ahead = g.within(G), (g + 1).within(G)
                    e = g + 2
                    stats = n == 1 and (e.within(G) or ahead)

                    def roots():
                        if stats:
                            wait(dve, s["root"], e)
                            V_.reciprocal(jy, jt).then_inc(s["norm"].sem, 1)

                    if now:
                        node_in(g)
                    if ahead:
                        if n == 1:
                            scaled(g + 1)
                        else:
                            sum_ends(g + 1)
                    if now:
                        weigh(g, 0)
                    if stats:
                        sums(e)
                    if ahead:
                        spread_z(g + 1, 0)
                    if stats:
                        mean(e)
                    if ahead:
                        spread_z(g + 1, 1)
                    if stats:
                        centre_rows(e)
                    if now:
                        weigh(g, 1)
                    if (g - 1).within(G):
                        scan(g - 1)
                    if stats:
                        variances(e)
                    if ahead:
                        spread_z(g + 1, 2)
                    if stats:
                        plus_eps(e)
                    if now:
                        weigh(g, 2)
                    if ahead:
                        spread_z(g + 1, 3)
                    if now:
                        add_knots(g, 0)
                        weigh(g, 3)
                    roots()
                    if now:
                        add_knots(g, 1)
                        node_out(g)

                each(dve, step, 2, 1)

            dve.wait_ge(s_w, WEIGHTS)
            dve.wait_ge(s_hat, 2 * K)
            conv(1)
            end_of(dve, cs[1]["comb"])
            layer2(*LAYER2[1])
            end_of(dve, m2["var"], MG)
            conv(2)

            roots(m2, 2)
            each(dve, lambda g: norm(g, m3, mx3), 0, 0, MG)

            V_.memset(mb[1][:, EG:EG + 1], 0.0).then_inc(s_mem, 1)
            V_.memset(sums[1][:, EG - 1:EG], 0.0).then_inc(s_mem, 1)
            dve.wait_ge(s_mem, 13)
            s1, s2, fin, nm = at["s1"], at["s2"], at["fin"], at["norm"]
            asum, amean, av, ay, a_t = (lns[:, k, :] for k in range(5))

            def x1_ends(g):
                wait_fill(dve, at["gathered"], g, 32 * TPG)
                X = x1[g.parity].rearrange("p (t e) c -> p t e c", e=2)
                wait(dve, fin, g - 2, "out")
                for slot, k in ((0, 1), (1, 0)):
                    V_.tensor_tensor(X[:, :, slot, :], gath[g.parity][:, :, k, 0:C], gath[g.parity][:, :, k, C:2 * C],
                                     ALU.add).then_inc(at["x1"].sem, 1)

            def centre_ends(g):
                wait(dve, at["x1"], g, "src")
                wait(dve, nm, g - 1, "eps")
                V_.tensor_reduce(asum, x1[g.parity], AX, ALU.add).then_inc(at["sum"].sem, 1)
                wait(dve, at["sum"], g)
                V_.tensor_scalar(amean, asum, -1.0 / C, None, ALU.mult).then_inc(nm.sem, 1)
                wait(dve, nm, g, "mean")
                wait(dve, at["xn"], g - 1)
                V_.tensor_tensor(lnc[:, :, :], x1[g.parity], amean.unsqueeze(2).broadcast_to([P, 2 * TPG, C]),
                                 ALU.add).then_inc(at["cen"].sem, 1)

            def variance(g):
                wait(dve, at["sq"], g)
                V_.tensor_reduce(asum, lnq[:, :, :], AX, ALU.add).then_inc(at["var"].sem, 1)

            def plus_eps(g):
                wait(dve, at["var"], g)
                V_.tensor_scalar(av, asum, 1.0 / C, EPS, ALU.mult, ALU.add).then_inc(nm.sem, 1)

            def normalise(g):
                wait(dve, nm, g, "n2c")
                wait(dve, at["xt"], g - 1)
                V_.tensor_tensor(xn.rearrange("p t (e c) -> p (t e) c", e=2), lnc[:, :, :],
                                 ay.unsqueeze(2).broadcast_to([P, 2 * TPG, C]), ALU.mult).then_inc(at["xn"].sem, 1)

            def cut_of(g):
                return restart[:, bass.ds(g.times(EG), EG)]

            def running_max(g):
                mx, before = mb[g.parity], mb[1 - g.parity]
                wait(dve, s1, g - 1, "step")
                V_.tensor_copy(mx[:, 0:1], before[:, EG:EG + 1]).then_inc(s1.sem, 1)
                wait(dve, s1, g, "carry")
                wait(dve, at["q"], g, "q1")
                V_.tensor_tensor_scan(mx[:, 1:EG + 1], cut_of(g), bank[2 + g.parity][:, :], mx[:, 0:1],
                                      ALU.add, ALU.max).then_inc(s1.sem, 1)

            def below_max(g):
                wait(dve, s1, g, "max")
                wait(dve, at["exp"], g - 1, "p")
                V_.tensor_tensor(lm[:, :], bank[2 + g.parity][:, :], mb[g.parity][:, 1:EG + 1], ALU.subtract)\
                    .then_inc(s1.sem, 1)

            def fall(g):
                wait(dve, at["exp"], g - 1, "d0")
                V_.tensor_tensor(dm[:, :], mb[g.parity][:, 0:EG], mb[g.parity][:, 1:EG + 1], ALU.subtract)\
                    .then_inc(s1.sem, 1)

            def cut_fall(g):
                wait(dve, s1, g, "step")
                V_.tensor_tensor(dm[:, :], dm[:, :], cut_of(g), ALU.add).then_inc(s1.sem, 1)

            def weigh_values(g):
                wait(dve, at["exp"], g, "p")
                wait(dve, at["q"], g, "q2")
                V_.tensor_tensor(pp[C:P, :], pp[C:P, :], bank[4 + g.parity][C:P, :], ALU.mult).then_inc(s2.sem, 1)

            def running_sums(g):
                wait(dve, s2, g, "pv")
                wait(dve, at["exp"], g, "d0")
                wait(dve, at["rt"], g - 2)
                V_.tensor_tensor_scan(sums[g.parity][:, :], d0[:, :], pp[:, :], sums[1 - g.parity][:, EG - 1:EG],
                                      ALU.mult, ALU.add).then_inc(s2.sem, 1)

            def finish(g):
                r = bank[6 + g.parity][:, :].rearrange("p (t h c) -> p t h c", h=2, c=C)
                wait(dve, at["rt"], g)
                wait(dve, fin, g - 1, "out")
                V_.reciprocal(rec[:, :, :], r[:, :, 0, :]).then_inc(fin.sem, 1)
                wait(dve, fin, g, "rec")
                V_.tensor_tensor(rec[:, :, :], rec[:, :, :], r[:, :, 1, :], ALU.mult).then_inc(fin.sem, 1)
                wait(dve, fin, g, "y")
                wait_fill(dve, at["scattered"], g - 2, 16 * TPG)
                V_.tensor_tensor(srow[g.parity][:, :, :], rec[:, :, :],
                                 x1[g.parity].rearrange("p (t e) c -> p t e c", e=2)[:, :, 0, :], ALU.add)\
                    .then_inc(fin.sem, 1)

            def step(g):
                now, ahead = g.within(G), (g + 1).within(G)
                e = g + 1

                def refine(*names):
                    if ahead:
                        for k in names:
                            newton(nm, e, k, av, ay, a_t)

                if (g - 1).within(G):
                    finish(g - 1)
                if ahead:
                    x1_ends(e)
                    centre_ends(e)
                if now:
                    running_max(g)
                    below_max(g)
                if ahead:
                    variance(e)
                if now:
                    fall(g)
                if ahead:
                    plus_eps(e)
                if now:
                    cut_fall(g)
                refine("seed", "n0a")
                if now:
                    weigh_values(g)
                refine("n0b", "n0c", "n1a")
                if now:
                    running_sums(g)
                refine("n1b", "n1c", "n2a", "n2b", "n2c")
                if ahead:
                    normalise(e)

            each(dve, step, 1, 1)


_INS = ["x", "src", "dst", "edge_attr_2", "edge_attr_3", "L0_gnn_W1", "L0_gnn_root1", "L0_gnn_bias1", "L0_gnn_W2",
        "L0_gnn_root2", "L0_gnn_bias2", "L1_gnn_Wd1", "L1_gnn_bd1", "L1_gnn_g1", "L1_gnn_b1", "L1_gnn_Wd2",
        "L1_gnn_bd2", "L1_gnn_g2", "L1_gnn_b2", "L1_gnn_W1", "L1_gnn_W2", "L1_gnn_W3"]


def kernel(**inputs):
    import numpy as _np
    import concourse.bacc as _bacc
    from concourse import mybir as _mybir
    from concourse.bass_utils import run_bass_kernel_spmd as _run

    nc = _bacc.Bacc("TRN2", target_bir_lowering=False, num_devices=1)
    arrays, args = {}, {}
    for name in _INS:
        v = _np.ascontiguousarray(inputs[name])
        arrays[f"in_{name}_dram"] = v
        args[name] = nc.dram_tensor(f"in_{name}_dram", v.shape, _mybir.dt.from_np(v.dtype), kind="ExternalInput").ap()
    shape = arrays["in_x_dram"].shape
    out = nc.dram_tensor("out_0_dram", shape, _mybir.dt.float32, kind="ExternalOutput").ap()
    build(nc, args, out)
    r = _run(nc, [arrays], core_ids=[0])
    return r.results[0]["out_0_dram"]
```
